# Optimizing a Trainium2 kernel written in Bass

```python
import numpy as np
import jax
import jax.numpy as jnp

def _softmax(x, axis=-1):
    return jax.nn.softmax(x, axis=axis)

def _gelu(x):
    return jax.nn.gelu(x, approximate=True)

def _silu(x):
    return jax.nn.silu(x)

def _sigmoid(x):
    return jax.nn.sigmoid(x)

def _layernorm(x, axis=-1, eps=1e-05):
    m = jnp.mean(x, axis=axis, keepdims=True)
    v = jnp.var(x, axis=axis, keepdims=True)
    return (x - m) / jnp.sqrt(v + eps)

def _scatter_add(tgt, idx, src, axis=0):
    return tgt.at[idx].add(src)

def _segment_sum(src, seg, n):
    return jax.ops.segment_sum(src, seg, n)
kernel_name = 'mk_cond_resid_d4_seqx_r8_d4e739'

def setup_inputs(seed: int=0):
    np.random.seed(seed)
    _w = jnp.asarray

    def _rec_inputs():
        import jax
        import jax.numpy as jnp
        _rk = jax.random.key(seed)
        x = 7.22e-05 + 1 * jax.random.normal(jax.random.fold_in(_rk, 1), (16, 128, 128), jnp.float32)
        _lenS = 128 - jax.random.randint(jax.random.fold_in(_rk, 7), (16,), 0, max(1, 128 // 4) + 1, jnp.int32)
        _lenS2 = 128 - jax.random.randint(jax.random.fold_in(_rk, 8), (16,), 0, max(1, 128 // 4) + 1, jnp.int32)
        cond_8 = jax.random.uniform(jax.random.fold_in(_rk, 11), (16, 8), jnp.float32, 0.0, 0.999837)
        return (x, cond_8)
    x, cond_8 = _rec_inputs()

    def _L0_cond_setup():
        import jax, jax.numpy as jnp
        import numpy as np
        key = jax.random.key(seed)
        k1, k2, k3, k4, k5 = jax.random.split(key, 5)
        B, N, T, O, G = (32, 32, 128, 128, 8)
        x = jax.random.normal(k1, (B, N, T), dtype=jnp.float32)
        y = jax.random.uniform(k2, (B, G), dtype=jnp.float32)
        weight = jax.random.normal(k3, (G, O, T), dtype=jnp.float32) * (1.0 / np.sqrt(T))
        mask = jax.random.uniform(k4, (O, T), dtype=jnp.float32)
        bias = jax.random.normal(k5, (O,), dtype=jnp.float32)
        return {'x': x, 'y': y, 'weight': weight, 'mask': mask, 'bias': bias}
    _L0_cond_all = _L0_cond_setup()
    _L0_cond_in = {k: v for k, v in _L0_cond_all.items() if k in ('weight', 'mask', 'bias')}
    del _L0_cond_all

    def _L1_cond_setup():
        import jax, jax.numpy as jnp
        import numpy as np
        TOP_K = 2
        NUM_MOE_LAYERS = 12

        def _gemma_mlp(x, gate_w, up_w, down_w):
            g = jnp.einsum('bsh,hi->bsi', x, gate_w)
            u = jnp.einsum('bsh,hi->bsi', x, up_w)
            return jnp.einsum('bsi,ih->bsh', jax.nn.gelu(g, approximate=True) * u, down_w)
        key = jax.random.key(seed)
        ks = jax.random.split(key, 8)
        B, S, H, I, E = (32, 32, 128, 512, 8)
        std = 0.02
        return {'x': jax.random.normal(ks[0], (B, S, H), jnp.float32), 'router_logits': jax.random.normal(ks[1], (B, E), jnp.float32), 'skill_gate': jax.random.normal(ks[2], (E, H, I), jnp.float32) * std, 'skill_up': jax.random.normal(ks[3], (E, H, I), jnp.float32) * std, 'skill_down': jax.random.normal(ks[4], (E, I, H), jnp.float32) * std, 'shared_gate': jax.random.normal(ks[5], (H, I), jnp.float32) * std, 'shared_up': jax.random.normal(ks[6], (H, I), jnp.float32) * std, 'shared_down': jax.random.normal(ks[7], (I, H), jnp.float32) * std}
    _L1_cond_all = _L1_cond_setup()
    _L1_cond_in = {k: v for k, v in _L1_cond_all.items() if k in ('skill_gate', 'skill_up', 'skill_down', 'shared_gate', 'shared_up', 'shared_down')}
    del _L1_cond_all

    def _L2_cond_setup():
        import jax, jax.numpy as jnp
        import numpy as np
        R = 16
        ALPHA = 32.0
        SCALING = ALPHA / R
        key = jax.random.key(seed)
        ks = jax.random.split(key, 6)
        B, T, C, O, E = (16, 1500, 128, 128, 8)
        x = jax.random.normal(ks[0], (B, T, C), dtype=jnp.float32)
        w = jax.random.uniform(ks[1], (B, E), dtype=jnp.float32)
        W_base = jax.random.normal(ks[2], (O, C), dtype=jnp.float32) * 0.02
        b_base = jax.random.normal(ks[3], (O,), dtype=jnp.float32) * 0.02
        As = jax.random.normal(ks[4], (E, R, C), dtype=jnp.float32) * 0.02
        Bs = jax.random.normal(ks[5], (E, O, R), dtype=jnp.float32) * 0.02
        return {'x': x, 'w': w, 'W_base': W_base, 'b_base': b_base, 'As': As, 'Bs': Bs}
    _L2_cond_all = _L2_cond_setup()
    _L2_cond_in = {k: v for k, v in _L2_cond_all.items() if k in ('W_base', 'b_base', 'As', 'Bs')}
    del _L2_cond_all

    def _L3_cond_setup():
        import jax, jax.numpy as jnp
        import numpy as np
        B, S, D = (16, 256, 128)
        E, H = (8, 256)
        key = jax.random.key(seed)
        ks = jax.random.split(key, 8)
        scale = 0.02
        x = jax.random.normal(ks[0], (B, S, D), dtype=jnp.float32)
        opcode_onehot = jax.random.uniform(ks[1], (B, E), dtype=jnp.float32)
        W_up = jax.random.normal(ks[2], (E, H, D), dtype=jnp.float32) * scale
        b_up = jnp.zeros((E, H), dtype=jnp.float32)
        W_gate = jax.random.normal(ks[3], (E, H, D), dtype=jnp.float32) * scale
        b_gate = jnp.zeros((E, H), dtype=jnp.float32)
        W_down = jax.random.normal(ks[4], (E, D, H), dtype=jnp.float32) * scale
        b_down = jnp.zeros((E, D), dtype=jnp.float32)
        return {'x': x, 'opcode_onehot': opcode_onehot, 'W_up': W_up, 'b_up': b_up, 'W_gate': W_gate, 'b_gate': b_gate, 'W_down': W_down, 'b_down': b_down}
    _L3_cond_all = _L3_cond_setup()
    _L3_cond_in = {k: v for k, v in _L3_cond_all.items() if k in ('W_up', 'b_up', 'W_gate', 'b_gate', 'W_down', 'b_down')}
    del _L3_cond_all
    return {'x': x, 'cond_8': cond_8, 'L0_cond_weight': _L0_cond_in['weight'], 'L0_cond_mask': _L0_cond_in['mask'], 'L0_cond_bias': _L0_cond_in['bias'], 'L1_cond_skill_gate': _L1_cond_in['skill_gate'], 'L1_cond_skill_up': _L1_cond_in['skill_up'], 'L1_cond_skill_down': _L1_cond_in['skill_down'], 'L1_cond_shared_gate': _L1_cond_in['shared_gate'], 'L1_cond_shared_up': _L1_cond_in['shared_up'], 'L1_cond_shared_down': _L1_cond_in['shared_down'], 'L2_cond_W_base': _L2_cond_in['W_base'], 'L2_cond_b_base': _L2_cond_in['b_base'], 'L2_cond_As': _L2_cond_in['As'], 'L2_cond_Bs': _L2_cond_in['Bs'], 'L3_cond_W_up': _L3_cond_in['W_up'], 'L3_cond_b_up': _L3_cond_in['b_up'], 'L3_cond_W_gate': _L3_cond_in['W_gate'], 'L3_cond_b_gate': _L3_cond_in['b_gate'], 'L3_cond_W_down': _L3_cond_in['W_down'], 'L3_cond_b_down': _L3_cond_in['b_down']}

def reference(x, cond_8, L0_cond_weight, L0_cond_mask, L0_cond_bias, L1_cond_skill_gate, L1_cond_skill_up, L1_cond_skill_down, L1_cond_shared_gate, L1_cond_shared_up, L1_cond_shared_down, L2_cond_W_base, L2_cond_b_base, L2_cond_As, L2_cond_Bs, L3_cond_W_up, L3_cond_b_up, L3_cond_W_gate, L3_cond_b_gate, L3_cond_W_down, L3_cond_b_down):
    import jax
    import jax.numpy as jnp

    def _L0_cond_ref(x, y, weight, mask, bias):
        import jax, jax.numpy as jnp
        import numpy as np
        masked_w = weight * mask[None, :, :]
        w_bot = jnp.einsum('bg,got->bot', y, masked_w)
        return jnp.einsum('bnt,bot->bno', x, w_bot) + bias

    def _L1_cond_ref(x, router_logits, skill_gate, skill_up, skill_down, shared_gate, shared_up, shared_down):
        import jax, jax.numpy as jnp
        import numpy as np
        TOP_K = 2
        NUM_MOE_LAYERS = 12

        def _gemma_mlp(x, gate_w, up_w, down_w):
            g = jnp.einsum('bsh,hi->bsi', x, gate_w)
            u = jnp.einsum('bsh,hi->bsi', x, up_w)
            return jnp.einsum('bsi,ih->bsh', jax.nn.gelu(g, approximate=True) * u, down_w)
        B = x.shape[0]
        E = skill_gate.shape[0]
        rw = jax.nn.softmax(router_logits.astype(jnp.float32), axis=-1)
        w, sel = jax.lax.top_k(rw, TOP_K)
        w = w / w.sum(axis=-1, keepdims=True)
        w = w.astype(x.dtype)
        scale = 1.0 / NUM_MOE_LAYERS
        w = scale * w + (1.0 - scale) * jax.lax.stop_gradient(w)
        dense_w = jnp.zeros((B, E), x.dtype).at[jnp.arange(B)[:, None], sel].add(w)

        def step(acc, params):
            g, u, d, we = params
            return (acc + we[:, None, None] * _gemma_mlp(x, g, u, d), None)
        out, _ = jax.lax.scan(step, jnp.zeros_like(x), (skill_gate, skill_up, skill_down, dense_w.T))
        out = out + _gemma_mlp(x, shared_gate, shared_up, shared_down)
        return out

    def _L2_cond_ref(x, w, W_base, b_base, As, Bs):
        import jax, jax.numpy as jnp
        import numpy as np
        R = 16
        ALPHA = 32.0
        SCALING = ALPHA / R
        out = jnp.einsum('btc,oc->bto', x, W_base) + b_base
        h = jnp.einsum('btc,erc->bter', x, As)
        lora = jnp.einsum('bter,eor,be->bto', h, Bs, w)
        return out + lora * SCALING

    def _L3_cond_ref(x, opcode_onehot, W_up, b_up, W_gate, b_gate, W_down, b_down):
        import jax, jax.numpy as jnp
        import numpy as np
        B, S, D = (16, 256, 128)
        E, H = (8, 256)
        expert = jnp.argmax(opcode_onehot, axis=-1)
        wu, bu = (W_up[expert], b_up[expert])
        wg, bg = (W_gate[expert], b_gate[expert])
        wd, bd = (W_down[expert], b_down[expert])
        up = jnp.einsum('bsd,bhd->bsh', x, wu) + bu[:, None, :]
        gate = jnp.einsum('bsd,bhd->bsh', x, wg) + bg[:, None, :]
        hidden = jax.nn.silu(up) * gate
        out = jnp.einsum('bsh,bdh->bsd', hidden, wd) + bd[:, None, :]
        return out
    x = x + _L0_cond_ref(x, cond_8, L0_cond_weight, L0_cond_mask, L0_cond_bias)
    x = x + _L1_cond_ref(x, cond_8, L1_cond_skill_gate, L1_cond_skill_up, L1_cond_skill_down, L1_cond_shared_gate, L1_cond_shared_up, L1_cond_shared_down)
    x = x + _L2_cond_ref(x, cond_8, L2_cond_W_base, L2_cond_b_base, L2_cond_As, L2_cond_Bs)
    x = x + _L3_cond_ref(x, cond_8, L3_cond_W_up, L3_cond_b_up, L3_cond_W_gate, L3_cond_b_gate, L3_cond_W_down, L3_cond_b_down)
    return x

_drawn_inputs = setup_inputs


def setup_inputs(seed=0):
    import zlib

    import numpy as np

    out = dict(_drawn_inputs(seed))
    spreads = {'L3_cond_b_up': (0.0, 0.8), 'L3_cond_b_gate': (0.0, 0.8), 'L3_cond_b_down': (0.0, 0.404)}
    factors = {'L1_cond_skill_gate': 3.815,
     'L1_cond_skill_up': 3.727,
     'L1_cond_skill_down': 3.656,
     'L1_cond_shared_gate': 2.845,
     'L1_cond_shared_up': 2.73,
     'L1_cond_shared_down': 2.805,
     'L2_cond_b_base': 4.949,
     'L3_cond_W_up': 3.669,
     'L3_cond_W_gate': 3.624,
     'L3_cond_W_down': 3.554}
    for name, (base, spread) in spreads.items():
        noise = np.random.default_rng([zlib.crc32(name.encode()), seed]).standard_normal(out[name].shape)
        drawn = base * np.exp(spread * noise) if base else spread * noise
        out[name] = jnp.asarray(drawn.astype(out[name].dtype))
    for name, factor in factors.items():
        out[name] = (out[name] * factor).astype(out[name].dtype)
    return out
```

```python
from contextlib import ExitStack

import concourse.bass as bass
from concourse import mybir

F32 = mybir.dt.float32
F32R = mybir.dt.float32r
I32 = mybir.dt.int32
ALU = mybir.AluOpType
ACT = mybir.ActivationFunctionType
AX = mybir.AxisListType

P = 128


def cond_resid_kernel(
    nc, xT_d, cond_d, condT_d, w0_d, mask_d, bias0_d,
    sk_gate_d, sk_up_d, sk_down_d, sh_gate_d, sh_up_d, sh_down_d,
    wbase_d, bbase_d, lora_a_d, lora_b_d,
    w3_d, b3_d, outT_d,
):
    TOK = xT_d.shape[1]
    B, E = cond_d.shape
    S = TOK // B
    I = sh_gate_d.shape[1]
    NC = I // P
    H3 = w3_d.shape[2] // 3
    NC3 = H3 // P
    GT = 512
    NG = TOK // GT
    BG = GT // S
    TOPK = 2
    PG = BG * TOPK
    NP = B * TOPK
    OI = P // E
    OB = P // OI
    LORA_SCALE = 2.0
    MOE_SCALE = 1.0 / 12
    W3 = 3 * H3
    NB3 = 2 * NC3 + 1
    assert S == P and B * E == P and NG == 4 and NC == 4 and NC3 == 2 and BG == 4

    with ExitStack() as ctx:
        def sb(name, shape, dt=F32):
            return ctx.enter_context(nc.sbuf_tensor(name, shape, dt))

        def sem(name):
            return ctx.enter_context(nc.semaphore(name))

        xT = sb("xT", [P, TOK])
        x_hi = sb("x_hi", [P, TOK], F32R)
        x_lo = sb("x_lo", [P, TOK], F32R)
        yT = sb("yT", [P, TOK])
        x3T = sb("x3T", [P, TOK])
        w0 = sb("w0", [P, OB * P])
        mask = sb("mask", [P, OB * P])
        cond_rep = sb("cond_rep", [P, B])
        cond_rep2 = sb("cond_rep2", [P, B])
        delta16 = sb("delta16", [P, OI])
        y_kron = sb("y_kron", [P, B, OI])
        wbotT = sb("wbotT", [P, B, P])
        ident = sb("ident", [P, P])
        biases = sb("biases", [P, 2])
        cond_bc = sb("cond_bc", [P, B, E])
        rev = sb("rev", [P, E])
        rev_i = sb("rev_i", [P, E], I32)
        r_a = sb("r_a", [P, B, E])
        r_b = sb("r_b", [P, B, E])
        r_w = sb("r_w", [P, B, E])
        r_w2 = sb("r_w2", [P, B, E])
        r_s = sb("r_s", [P, 8, B])
        pair_w0 = sb("pair_w0", [P, B, TOPK])
        pair_w1 = sb("pair_w1", [P, B, TOPK])
        pair_w = sb("pair_w", [P, B, TOPK])
        pair_e = sb("pair_e", [P, B, TOPK], I32)
        best_e = sb("best_e", [P, B], I32)
        sh_raw = sb("sh_raw", [P, 3, I])
        sh_hi = sb("sh_hi", [P, 3, I], F32R)
        sh_lo = sb("sh_lo", [P, 3, I], F32R)
        gelu_s = sb("gelu_s", [P, 2, GT])
        prod_s = sb("prod_s", [P, 2, GT])
        prod_hi = sb("prod_hi", [P, 2, GT], F32R)
        prod_lo = sb("prod_lo", [P, 2, GT], F32R)
        sk_gu = sb("sk_gu", [P, E, 2 * I])
        sk_dn = sb("sk_dn", [P, E, I])
        pair_gu = sb("pair_gu", [P, 2, 2 * I])
        pair_dn = sb("pair_dn", [P, 2, I])
        l2_raw = sb("l2_raw", [P, 3, P])
        l2_hi = sb("l2_hi", [P, 2, P], F32R)
        l2_lo = sb("l2_lo", [P, 2, P], F32R)
        lora_h = sb("lora_h", [P, BG, S])
        w3 = sb("w3", [P, E, W3])
        b3 = sb("b3", [P, E, NB3])
        batch_w3 = sb("batch_w3", [P, BG, W3])
        batch_b3 = sb("batch_b3", [P, BG, NB3])
        silu_s = sb("silu_s", [P, 2, H3])
        hid3 = sb("hid3", [P, 2, H3])

        gu = ctx.enter_context(nc.psum_tensor("gu", [P, 4, GT], F32))
        yy = ctx.enter_context(nc.psum_tensor("yy", [P, 4, GT], F32))

        cond_in, w0_in, mask_in, x_in = sem("cond_in"), sem("w0_in"), sem("mask_in"), sem("x_in")
        shgu_in, shdn_in, l2_in, skill_in, w3_in = (
            sem("shgu_in"), sem("shdn_in"), sem("l2_in"), sem("skill_in"), sem("w3_in"))
        out_stored = sem("out_stored")
        pool_const = sem("pool_const")
        route_step = sem("route_step")
        exp_ready, exp_in_ready, route_ready = sem("exp_ready"), sem("exp_in_ready"), sem("route_ready")
        setup_dve = sem("setup_dve")
        kron_ready, masked_ready = sem("kron_ready"), sem("masked_ready")
        wbot_done, wbot_act, wbot_dve = sem("wbot_done"), sem("wbot_act"), sem("wbot_dve")
        l0_done, x1_done, x1hi_done, x1lo_dve, x1lo_pool = (
            sem("l0_done"), sem("x1_done"), sem("x1hi_done"), sem("x1lo_dve"), sem("x1lo_pool"))
        whi_done, wlo_done = sem("whi_done"), sem("wlo_done")
        sh_g_done, sh_u_done, sh_dn_done = sem("sh_g_done"), sem("sh_u_done"), sem("sh_dn_done")
        sh_gelu_done, sh_prod_done, sh_hi_done, sh_lo_done, sh_y_done = (
            sem("sh_gelu_done"), sem("sh_prod_done"), sem("sh_hi_done"), sem("sh_lo_done"), sem("sh_y_done"))
        gu_copied, dn_copied = sem("gu_copied"), sem("dn_copied")
        ex_g_done, ex_u_done, ex_dn_done = sem("ex_g_done"), sem("ex_u_done"), sem("ex_dn_done")
        ex_gelu_done, ex_prod_done, x2_done = sem("ex_gelu_done"), sem("ex_prod_done"), sem("x2_done")
        l2_hi_done, l2_lo_done, l2_h_done, l2_hs_done, l2_x_done, x3_done = (
            sem("l2_hi_done"), sem("l2_lo_done"), sem("l2_h_done"), sem("l2_hs_done"), sem("l2_x_done"), sem("x3_done"))
        w3_copied, b3_copied = sem("w3_copied"), sem("b3_copied")
        up3_done, gate3_done, dn3_done = sem("up3_done"), sem("gate3_done"), sem("dn3_done")
        silu_done, hid3_done, out_done = sem("silu_done"), sem("hid3_done"), sem("out_done")

        N_SKILL = 3 * E
        N_W3 = 2

        def cols(i, n):
            return bass.ds(i * n, n)

        pair_w_cols = pair_w[:].rearrange("p b k -> p (b k)")
        pair_e_cols = pair_e[:].rearrange("p b k -> p (b k)")
        xT_b = xT[:]
        block = ctx.enter_context(nc.Block())

        @block.sync
        def _(sp):
            sp.dma_start(cond_rep[:], bass.AP(condT_d.tensor, 0, [[B, E], [0, OI], [1, B]])).then_inc(cond_in, 16)
            sp.dma_start(w0[:], w0_d).then_inc(w0_in, 16)
            for g in range(NG):
                sp.dma_start(xT[:, g * GT:(g + 1) * GT], xT_d[:, g * GT:(g + 1) * GT]).then_inc(x_in, 16)
            sp.dma_start(sh_raw[:, 0, :], sh_gate_d).then_inc(shgu_in, 16)
            sp.dma_start(sh_raw[:, 1, :], sh_up_d).then_inc(shgu_in, 16)
            sp.dma_start(sh_raw[:, 2, :].rearrange("p (c h) -> p c h", c=NC),
                         sh_down_d.rearrange("(c p) h -> p c h", p=P)).then_inc(shdn_in, 16)
            sp.dma_start(l2_raw[:, 0, :], wbase_d).then_inc(l2_in, 16)
            sp.dma_start(l2_raw[:, 1, :], lora_a_d).then_inc(l2_in, 16)
            sp.dma_start(l2_raw[:, 2, :], lora_b_d).then_inc(l2_in, 16)
            for e in range(E):
                sp.dma_start(sk_gu[:, e, 0:I], sk_gate_d[e]).then_inc(skill_in, 16)
                sp.dma_start(sk_gu[:, e, I:2 * I], sk_up_d[e]).then_inc(skill_in, 16)
                sp.dma_start(sk_dn[:, e, :].rearrange("p (c h) -> p c h", c=NC),
                             sk_down_d[e].rearrange("(c p) h -> p c h", p=P)).then_inc(skill_in, 16)
            sp.dma_start(w3[:], w3_d).then_inc(w3_in, 16)
            sp.dma_start(b3[:], b3_d).then_inc(w3_in, 16)
            for g in range(NG):
                sp.wait_ge(out_done, (g + 1) * BG)
                sp.dma_start(outT_d[:, g * GT:(g + 1) * GT], x3T[:, g * GT:(g + 1) * GT]).then_inc(out_stored, 16)
            sp.wait_ge(out_stored, 16 * NG)

        @block.gpsimd
        def _(pool):
            pool.memset(ident[:], 0.0).then_inc(pool_const, 1)
            pool.iota(rev_i[:], [[-1, E]], base=E, channel_multiplier=0).then_inc(pool_const, 1)
            pool.wait_ge(pool_const, 2)
            pool.affine_select(out=ident[:], in_=ident[:], compare_op=ALU.not_equal, fill=1.0, base=0,
                               pattern=[[-1, P]], channel_multiplier=1).then_inc(pool_const, 1)
            for g in range(1, NG):
                c = slice(g * GT, (g + 1) * GT)
                pool.wait_ge(x1hi_done, g + 1)
                pool.tensor_tensor(x_lo[:, c], xT[:, c], x_hi[:, c].bitcast(F32), ALU.subtract).then_inc(x1lo_pool, 1)

        @block.tensor
        def _(pe):
            def split3(out, w_hi, w_lo, m_hi, m_lo, start, stop):
                pe.matmul(out, w_hi, m_hi, start=start, stop=False)
                pe.matmul(out, w_hi, m_lo, start=False, stop=False)
                return pe.matmul(out, w_lo, m_hi, start=False, stop=stop)

            pe.wait_ge(kron_ready, 1)
            pe.wait_ge(masked_ready, 1)
            for ob in range(OB):
                pe.matmul(gu[:, ob // 2, (ob % 2) * B * OI:(ob % 2 + 1) * B * OI], w0[:, ob * P:(ob + 1) * P],
                          y_kron[:].rearrange("p b o -> p (b o)"), start=True, stop=True).then_inc(wbot_done, 1)
            pe.wait_ge(wbot_act, 2)
            pe.wait_ge(wbot_dve, 2)
            for g in range(NG):
                pe.wait_ge(x_in, 16 * NG)
                for b in range(g * BG, (g + 1) * BG):
                    mm = pe.matmul(yy[:, g, (b % BG) * S:(b % BG + 1) * S], wbotT[:, b, :], xT[:, b * S:(b + 1) * S],
                                   start=True, stop=True)
                mm.then_inc(l0_done, 1)

            def shared_up(g, c, first):
                q = g * NC + c
                tok = bass.ds(g * GT, GT)
                ch = slice(c * P, (c + 1) * P)
                if not (first and c < 2):
                    pe.wait_ge(sh_gelu_done, q - 1)
                split3(gu[:, c % 2, :], sh_hi[:, 0, ch], sh_lo[:, 0, ch], x_hi[:, tok], x_lo[:, tok],
                       True, True).then_inc(sh_g_done, 1)
                if not (first and c < 2):
                    pe.wait_ge(sh_prod_done, q - 1)
                split3(gu[:, 2 + c % 2, :], sh_hi[:, 1, ch], sh_lo[:, 1, ch], x_hi[:, tok], x_lo[:, tok],
                       True, True).then_inc(sh_u_done, 1)

            def shared_down(g, c):
                q = g * NC + c
                ch = slice(c * P, (c + 1) * P)
                pe.wait_ge(sh_hi_done, q + 1)
                pe.wait_ge(sh_lo_done, q + 1)
                out = yy[:, bass.ds(g, 1), :].rearrange("p a n -> p (a n)")
                split3(out, sh_hi[:, 2, ch], sh_lo[:, 2, ch], prod_hi[:, c % 2, :], prod_lo[:, c % 2, :],
                       c == 0, c == NC - 1).then_inc(sh_dn_done, 1)

            def shared_group(g, first):
                pe.wait_ge(x1hi_done, g + 1)
                if first:
                    pe.wait_ge(x1lo_dve, 1)
                else:
                    pe.wait_ge(x1lo_pool, g)
                for c in range(NC):
                    shared_up(g, c, first)
                    if c >= 2:
                        shared_down(g, c - 2)
                    elif not first:
                        shared_down(g - 1, c + NC - 2)

            pe.wait_ge(whi_done, 2)
            pe.wait_ge(wlo_done, 2)
            shared_group(0, True)
            with pe.Fori(1, NG) as g:
                shared_group(g, False)

            def expert_up(b, k, par, first):
                p = b * TOPK + k
                pe.wait_ge(gu_copied, p + 1)
                tok = bass.ds(b * S, S)
                if first and par < 2:
                    pe.wait_ge(sh_gelu_done, NG * NC - 1 + par)
                else:
                    pe.wait_ge(ex_gelu_done, p - 1)
                for c in range(NC):
                    mm = pe.matmul(gu[:, k, c * S:(c + 1) * S], pair_gu[:, k, c * P:(c + 1) * P], xT[:, tok],
                                   start=True, stop=True)
                mm.then_inc(ex_g_done, 1)
                if first and par < 2:
                    pe.wait_ge(sh_prod_done, NG * NC - 1 + par)
                else:
                    pe.wait_ge(ex_prod_done, p - 1)
                for c in range(NC):
                    mm = pe.matmul(gu[:, 2 + k, c * S:(c + 1) * S], pair_gu[:, k, I + c * P:I + (c + 1) * P],
                                   xT[:, tok], start=True, stop=True)
                mm.then_inc(ex_u_done, 1)

            def expert_down(b, k, ypar, first):
                p = b * TOPK + k
                pe.wait_ge(ex_prod_done, p + 1)
                pe.wait_ge(dn_copied, p + 1)
                if k == 0:
                    if first:
                        pe.wait_ge(sh_y_done, ypar + 1)
                    else:
                        pe.wait_ge(x2_done, b - 1)
                for c in range(NC):
                    mm = pe.matmul(yy[:, ypar, 0:S], pair_dn[:, k, c * P:(c + 1) * P],
                                   prod_s[:, k, c * S:(c + 1) * S],
                                   start=(k == 0 and c == 0), stop=(k == TOPK - 1 and c == NC - 1))
                mm.then_inc(ex_dn_done, 1)

            def lora_in(g, first):
                tok = bass.ds(g * GT, GT)
                pe.wait_ge(l2_hi_done, g + 1)
                pe.wait_ge(l2_lo_done, g + 1)
                if first:
                    pe.wait_ge(sh_y_done, NG)
                    pe.wait_ge(whi_done, 4)
                    pe.wait_ge(wlo_done, 4)
                else:
                    pe.wait_ge(l2_hs_done, g)
                split3(yy[:, 2, :], l2_hi[:, 1, :], l2_lo[:, 1, :], x_hi[:, tok], x_lo[:, tok],
                       True, True).then_inc(l2_h_done, 1)
                if not first:
                    pe.wait_ge(x3_done, g)
                split3(yy[:, 3, :], l2_hi[:, 0, :], l2_lo[:, 0, :], x_hi[:, tok], x_lo[:, tok], True, False)

            def lora_out(g):
                pe.wait_ge(l2_hs_done, g + 1)
                pe.matmul(yy[:, 3, :], l2_raw[:, 2, :], lora_h[:].rearrange("p b s -> p (b s)"),
                          start=False, stop=True).then_inc(l2_x_done, 1)

            def expert_group(g, first, l2_first=False):
                for j in range(PG):
                    b, k = g * BG + j // TOPK, j % TOPK
                    if not (first and j == 0):
                        expert_up(b, k, j, first)
                    if j >= 1:
                        jb, jk = (j - 1) // TOPK, (j - 1) % TOPK
                        expert_down(g * BG + jb, jk, jb % 2, first and jb < 2)
                    elif not first:
                        expert_down(g * BG - 1, TOPK - 1, (BG - 1) % 2, False)
                    if not first and j == 4:
                        lora_in(g - 1, l2_first)
                    if not first and j == 6:
                        lora_out(g - 1)

            shared_down(NG - 1, NC - 2)
            expert_up(0, 0, 0, True)
            shared_down(NG - 1, NC - 1)
            expert_group(0, True)
            expert_group(1, False, l2_first=True)
            with pe.Fori(2, NG) as g:
                expert_group(g, False)

            def up3(b, j, first):
                tok = bass.ds(b * S, S)
                pe.wait_ge(w3_copied, b + 1)
                if first and j < 2:
                    pe.wait_ge(ex_gelu_done, NP)
                    pe.wait_ge(x3_done, 1)
                else:
                    pe.wait_ge(silu_done, (b - 1) * NC3)
                for c in range(NC3):
                    mm = pe.matmul(gu[:, j % 2, c * S:(c + 1) * S], batch_w3[:, j, c * P:(c + 1) * P], xT3(tok),
                                   start=True, stop=True)
                mm.then_inc(up3_done, 1)
                if first and j < 2:
                    pe.wait_ge(ex_prod_done, NP)
                else:
                    pe.wait_ge(hid3_done, (b - 1) * NC3)
                for c in range(NC3):
                    mm = pe.matmul(gu[:, 2 + j % 2, c * S:(c + 1) * S], batch_w3[:, j, H3 + c * P:H3 + (c + 1) * P],
                                   xT3(tok), start=True, stop=True)
                mm.then_inc(gate3_done, 1)

            def xT3(tok):
                return x3T[:, tok]

            def down3(b, j, first):
                if first and j < 2:
                    pe.wait_ge(x2_done, B - 1 + j)
                else:
                    pe.wait_ge(out_done, b - 1)
                for c in range(NC3):
                    pe.wait_ge(hid3_done, b * NC3 + c + 1)
                    mm = pe.matmul(yy[:, j % 2, 0:S], batch_w3[:, j, 2 * H3 + c * P:2 * H3 + (c + 1) * P],
                                   hid3[:, j % 2, c * S:(c + 1) * S], start=(c == 0), stop=(c == NC3 - 1))
                mm.then_inc(dn3_done, 1)

            def l3_group(g, first):
                if not first:
                    pe.wait_ge(x3_done, g + 1)
                for j in range(BG):
                    b = g * BG + j
                    up3(b, j, first)
                    if first and j == 0:
                        expert_down(B - 1, TOPK - 1, (B - 1) % 2, False)
                    elif first and j == 2:
                        down3(1, 1, True)
                        lora_in(NG - 1, False)
                    elif j >= 1:
                        down3(b - 1, j - 1, first)
                    else:
                        down3(b - 1, BG - 1, False)
                    if first and j == 3:
                        lora_out(NG - 1)

            l3_group(0, True)
            with pe.Fori(1, NG) as g:
                l3_group(g, False)
            down3(B - 1, BG - 1, False)

        @block.scalar
        def _(act):
            act.dma_start(cond_bc[:].rearrange("p b e -> p (b e)"),
                          bass.AP(cond_d.tensor, 0, [[0, P], [1, B * E]])).then_inc(cond_in, 16)
            act.dma_start(mask[:], bass.AP(mask_d.tensor, 0, [[0, E], [OB * P, OI], [1, OB * P]])).then_inc(mask_in, 16)
            act.dma_start(biases[:, 0:1], bias0_d).then_inc(l2_in, 16)
            act.dma_start(biases[:, 1:2], bbase_d).then_inc(l2_in, 16)
            act.wait_ge(exp_in_ready, 1)
            act.activation(r_b[:], r_a[:], ACT.Exp).then_inc(exp_ready, 1)
            act.wait_ge(shgu_in, 32)
            act.activation(sh_hi[:, 0, :], sh_raw[:, 0, :], ACT.Copy).then_inc(whi_done, 1)
            act.activation(sh_hi[:, 1, :], sh_raw[:, 1, :], ACT.Copy).then_inc(whi_done, 1)
            for k in (0, 2):
                act.wait_ge(wbot_done, 2 * k + 2)
                act.activation(wbotT[:, :, 2 * k * OI:(2 * k + 2) * OI].rearrange("p b (a o) -> p a b o", a=2),
                               gu[:, k, :].rearrange("p (a b o) -> p a b o", a=2, b=B), ACT.Copy).then_inc(wbot_act, 1)
            for g in range(NG):
                c = slice(g * GT, (g + 1) * GT)
                act.wait_ge(x1_done, g + 1)
                act.activation(x_hi[:, c], xT[:, c], ACT.Copy).then_inc(x1hi_done, 1)
                if g == 0:
                    act.wait_ge(shdn_in, 16)
                    act.activation(sh_hi[:, 2, :], sh_raw[:, 2, :], ACT.Copy).then_inc(whi_done, 1)
            act.wait_ge(l2_in, 16 * 5)
            act.activation(l2_hi[:], l2_raw[:, 0:2, :], ACT.Copy).then_inc(whi_done, 1)

            def shared_gelu(q, par, first):
                act.wait_ge(sh_g_done, q + 1)
                if not first:
                    act.wait_ge(sh_prod_done, q - 1)
                act.activation(gelu_s[:, par, :], gu[:, par, :], ACT.Gelu_apprx_tanh).then_inc(sh_gelu_done, 1)

            def shared_hi(q, par, first):
                act.wait_ge(sh_prod_done, q + 1)
                if not first:
                    act.wait_ge(sh_dn_done, q - 1)
                act.activation(prod_hi[:, par, :], prod_s[:, par, :], ACT.Copy).then_inc(sh_hi_done, 1)

            def shared_group(g, first):
                for c in range(NC):
                    shared_gelu(g * NC + c, c % 2, first and c < 2)
                    if not (first and c == 0):
                        shared_hi(g * NC + c - 1, (c - 1) % 2, first and c < 3)

            shared_group(0, True)
            with act.Fori(1, NG) as g:
                shared_group(g, False)

            def copy_down(p, k, first):
                if not first:
                    act.wait_ge(ex_dn_done, p - 1)
                e = act.value_load(pair_e_cols[0:1, bass.ds(p, 1)], min_val=0, max_val=E - 1)
                act.activation(pair_dn[:, k, :], sk_dn[:, bass.ds(e, 1), :].rearrange("p a n -> p (a n)"),
                               ACT.Copy).then_inc(dn_copied, 1)

            def expert_gelu(p, k, first):
                act.wait_ge(ex_g_done, p + 1)
                if not first:
                    act.wait_ge(ex_prod_done, p - 1)
                act.activation(gelu_s[:, k, :], gu[:, k, :], ACT.Gelu_apprx_tanh).then_inc(ex_gelu_done, 1)

            def l2_split(g):
                c = bass.ds(g * GT, GT)
                act.wait_ge(x2_done, (g + 1) * BG)
                act.activation(x_hi[:, c], yT[:, c], ACT.Copy).then_inc(l2_hi_done, 1)

            def expert_group(g, first):
                for j in range(PG):
                    if not (first and j == 0):
                        expert_gelu(g * PG + j - 1, (j - 1) % TOPK, first and j < 3)
                        copy_down(g * PG + j, j % TOPK, first and j < 2)
                    if not first and j == 2:
                        l2_split(g - 1)

            act.wait_ge(route_ready, 1)
            act.wait_ge(skill_in, 16 * N_SKILL)
            copy_down(0, 0, True)
            shared_hi(NG * NC - 1, 1, False)
            expert_group(0, True)
            with act.Fori(1, NG) as g:
                expert_group(g, False)

            def copy_b3(b, j, first):
                if not first:
                    act.wait_ge(out_done, b - BG + 1)
                e = act.value_load(best_e[0:1, bass.ds(b, 1)], min_val=0, max_val=E - 1)
                act.activation(batch_b3[:, j, :], b3[:, bass.ds(e, 1), :].rearrange("p a n -> p (a n)"),
                               ACT.Copy).then_inc(b3_copied, 1)

            def silu3(b, j, first):
                act.wait_ge(up3_done, b + 1)
                act.wait_ge(b3_copied, b + 1)
                if not first:
                    act.wait_ge(hid3_done, (b - 1) * NC3)
                for c in range(NC3):
                    cs = slice(c * S, (c + 1) * S)
                    act.activation(silu_s[:, j % 2, cs], gu[:, j % 2, cs], ACT.Silu,
                                   bias=batch_b3[:, j, c:c + 1]).then_inc(silu_done, 1)

            def l3_group(g, first):
                for j in range(BG):
                    b = g * BG + j
                    copy_b3(b, j, first)
                    if not (first and j == 0):
                        silu3(b - 1, (j - 1) % BG, first and j < 3)
                    if first and j == 0:
                        l2_split(NG - 1)

            act.wait_ge(w3_in, 16 * N_W3)
            expert_gelu(NP - 1, TOPK - 1, False)
            l3_group(0, True)
            with act.Fori(1, NG) as g:
                l3_group(g, False)
            silu3(B - 1, BG - 1, False)

        @block.vector
        def _(dve):
            step = [0]

            def link(ins):
                step[0] += 1
                ins.then_inc(route_step, 1)
                dve.wait_ge(route_step, step[0])

            def over_e(a):
                return a.rearrange("p (b o) -> p b o", o=1).broadcast_to([P, B, E])

            def over_b(a):
                return a.rearrange("p (o e) -> p o e", o=1).broadcast_to([P, B, E])

            dve.wait_ge(pool_const, 3)
            link(dve.tensor_reduce(delta16[:], ident[:].rearrange("p (k o) -> p o k", o=OI), AX.X, ALU.add))
            link(dve.tensor_copy(rev[:], rev_i[:]))
            dve.wait_ge(cond_in, 32)
            dve.tensor_tensor(y_kron[:], cond_rep[:].rearrange("p (b o) -> p b o", o=1).broadcast_to([P, B, OI]),
                              delta16[:].rearrange("p (b o) -> p b o", b=1).broadcast_to([P, B, OI]),
                              ALU.mult).then_inc(kron_ready, 1)
            cmax, esum, rsum, best, bestr, sec, secr, topr = (r_s[:, i, :] for i in range(8))
            link(dve.tensor_reduce(cmax, cond_bc[:], AX.X, ALU.max))
            dve.tensor_tensor(r_a[:], cond_bc[:], over_e(cmax), ALU.subtract).then_inc(exp_in_ready, 1)
            dve.wait_ge(w0_in, 16)
            dve.wait_ge(mask_in, 16)
            dve.tensor_tensor(w0[:], w0[:], mask[:], ALU.mult).then_inc(masked_ready, 1)
            dve.tensor_scalar(cond_rep2[:], cond_rep[:], LORA_SCALE, None, ALU.mult).then_inc(setup_dve, 1)
            dve.wait_ge(exp_ready, 1)
            link(dve.tensor_tensor(r_w2[:], cond_bc[:], over_e(cmax), ALU.is_equal))
            link(dve.tensor_tensor(r_w2[:], r_w2[:], over_b(rev[:]), ALU.mult))
            link(dve.tensor_reduce(topr, r_w2[:], AX.X, ALU.max))
            link(dve.tensor_scalar(best_e[:], topr, -1.0, float(E), ALU.mult, ALU.add))
            link(dve.tensor_reduce(esum, r_b[:], AX.X, ALU.add))
            link(dve.reciprocal(rsum, esum))
            link(dve.tensor_tensor(r_w[:], r_b[:], over_e(rsum), ALU.mult))

            def wbot_out(k):
                dve.wait_ge(wbot_done, 2 * k + 2)
                dve.tensor_copy(wbotT[:, :, 2 * k * OI:(2 * k + 2) * OI].rearrange("p b (a o) -> p a b o", a=2),
                                gu[:, k, :].rearrange("p (a b o) -> p a b o", a=2, b=B)).then_inc(wbot_dve, 1)

            def w_lo(k, n):
                dve.wait_ge(whi_done, n)
                dve.tensor_tensor(sh_lo[:, k, :], sh_raw[:, k, :], sh_hi[:, k, :].bitcast(F32),
                                  ALU.subtract).then_inc(wlo_done, 1)

            link(dve.tensor_reduce(best, r_w[:], AX.X, ALU.max))
            link(dve.tensor_tensor(r_a[:], r_w[:], over_e(best), ALU.is_equal))
            link(dve.tensor_tensor(r_a[:], r_a[:], over_b(rev[:]), ALU.mult))
            link(dve.tensor_reduce(bestr, r_a[:], AX.X, ALU.max))
            wbot_out(1)
            w_lo(0, 1)
            w_lo(1, 2)
            wbot_out(3)
            dve.wait_ge(l2_in, 16 * 5)
            for g in range(NG):
                c = slice(g * GT, (g + 1) * GT)
                dve.wait_ge(l0_done, g + 1)
                dve.scalar_tensor_tensor(out=xT[:, c], in0=yy[:, g, :], scalar=biases[:, 0:1], in1=xT[:, c],
                                         op0=ALU.add, op1=ALU.add).then_inc(x1_done, 1)
                if g == 0:
                    dve.wait_ge(x1hi_done, 1)
                    dve.tensor_tensor(x_lo[:, c], xT[:, c], x_hi[:, c].bitcast(F32), ALU.subtract).then_inc(x1lo_dve, 1)
            w_lo(2, 3)

            def shared_prod(q, par, first):
                dve.wait_ge(sh_gelu_done, q + 1)
                dve.wait_ge(sh_u_done, q + 1)
                if not first:
                    dve.wait_ge(sh_lo_done, q - 1)
                dve.tensor_tensor(prod_s[:, par, :], gelu_s[:, par, :], gu[:, 2 + par, :],
                                  ALU.mult).then_inc(sh_prod_done, 1)

            def shared_lo(q, par, first):
                dve.wait_ge(sh_hi_done, q + 1)
                if not first:
                    dve.wait_ge(sh_dn_done, q - 1)
                dve.tensor_tensor(prod_lo[:, par, :], prod_s[:, par, :], prod_hi[:, par, :].bitcast(F32),
                                  ALU.subtract).then_inc(sh_lo_done, 1)

            def shared_y(g):
                c = bass.ds(g * GT, GT)
                dve.wait_ge(sh_dn_done, (g + 1) * NC)
                dve.tensor_tensor(yT[:, c], yy[:, bass.ds(g, 1), :].rearrange("p a n -> p (a n)"), xT[:, c],
                                  ALU.add).then_inc(sh_y_done, 1)

            def shared_group(g, first):
                for c in range(NC):
                    shared_prod(g * NC + c, c % 2, first and c < 2)
                    if not (first and c == 0):
                        shared_lo(g * NC + c - 1, (c - 1) % 2, first and c < 3)
                    if not first and c == 2:
                        shared_y(g - 1)

            shared_group(0, True)
            link(dve.tensor_tensor(r_a[:], over_b(rev[:]), over_e(bestr), ALU.is_equal))
            link(dve.scalar_tensor_tensor(out=r_w2[:], in0=r_a[:], scalar=-2.0, in1=r_w[:], op0=ALU.mult, op1=ALU.add))
            link(dve.tensor_reduce(sec, r_w2[:], AX.X, ALU.max))
            link(dve.tensor_tensor(r_a[:], r_w2[:], over_e(sec), ALU.is_equal))
            link(dve.tensor_tensor(r_a[:], r_a[:], over_b(rev[:]), ALU.mult))
            link(dve.tensor_reduce(secr, r_a[:], AX.X, ALU.max))
            link(dve.tensor_scalar(pair_e[:, :, 0], bestr, -1.0, float(E), ALU.mult, ALU.add))
            link(dve.tensor_scalar(pair_e[:, :, 1], secr, -1.0, float(E), ALU.mult, ALU.add))
            link(dve.tensor_tensor(esum, best, sec, ALU.add))
            link(dve.reciprocal(rsum, esum))
            link(dve.tensor_tensor(pair_w0[:, :, 0], best, rsum, ALU.mult))
            link(dve.tensor_tensor(pair_w0[:, :, 1], sec, rsum, ALU.mult))
            link(dve.tensor_scalar(pair_w1[:], pair_w0[:], 1.0 - MOE_SCALE, None, ALU.mult))
            dve.scalar_tensor_tensor(out=pair_w[:], in0=pair_w0[:], scalar=MOE_SCALE, in1=pair_w1[:],
                                     op0=ALU.mult, op1=ALU.add).then_inc(route_ready, 1)
            dve.wait_ge(whi_done, 4)
            dve.tensor_tensor(l2_lo[:], l2_raw[:, 0:2, :], l2_hi[:].bitcast(F32), ALU.subtract).then_inc(wlo_done, 1)
            with dve.Fori(1, NG) as g:
                shared_group(g, False)

            def copy_gu(p, k, first):
                if not first:
                    dve.wait_ge(ex_u_done, p - 1)
                e = dve.value_load(pair_e_cols[0:1, bass.ds(p, 1)], min_val=0, max_val=E - 1)
                dve.tensor_copy(pair_gu[:, k, :], sk_gu[:, bass.ds(e, 1), :].rearrange("p a n -> p (a n)")
                                ).then_inc(gu_copied, 1)

            def expert_prod(p, k, first):
                dve.wait_ge(ex_gelu_done, p + 1)
                dve.wait_ge(ex_u_done, p + 1)
                if first:
                    dve.wait_ge(sh_lo_done, NG * NC)
                else:
                    dve.wait_ge(ex_dn_done, p - 1)
                dve.scalar_tensor_tensor(out=prod_s[:, k, :], in0=gelu_s[:, k, :], scalar=pair_w_cols[:, bass.ds(p, 1)],
                                         in1=gu[:, 2 + k, :], op0=ALU.mult, op1=ALU.mult).then_inc(ex_prod_done, 1)

            def x2_out(b, ypar):
                c = bass.ds(b * S, S)
                dve.wait_ge(ex_dn_done, (b + 1) * TOPK)
                dve.tensor_tensor(yT[:, c], yy[:, ypar, 0:S], yT[:, c], ALU.add).then_inc(x2_done, 1)

            def l2_lo_part(g):
                c = bass.ds(g * GT, GT)
                dve.wait_ge(l2_hi_done, g + 1)
                dve.tensor_tensor(x_lo[:, c], yT[:, c], x_hi[:, c].bitcast(F32), ALU.subtract).then_inc(l2_lo_done, 1)

            def l2_scale(g, first):
                dve.wait_ge(l2_h_done, g + 1)
                if not first:
                    dve.wait_ge(l2_x_done, g)
                dve.tensor_tensor(lora_h[:], yy[:, 2, :].rearrange("p (b s) -> p b s", s=S),
                                  cond_rep2[:, bass.ds(g * BG, BG)].rearrange("p (b o) -> p b o", o=1)
                                  .broadcast_to([P, BG, S]), ALU.mult).then_inc(l2_hs_done, 1)

            def x3_out(g):
                c = bass.ds(g * GT, GT)
                dve.wait_ge(l2_x_done, g + 1)
                dve.scalar_tensor_tensor(out=x3T[:, c], in0=yy[:, 3, :], scalar=biases[:, 1:2], in1=yT[:, c],
                                         op0=ALU.add, op1=ALU.add).then_inc(x3_done, 1)

            def expert_group(g, first, l2_first=False):
                for j in range(PG):
                    p = g * PG + j
                    if not (first and j == 0):
                        copy_gu(p, j % TOPK, first and j < 2)
                        expert_prod(p - 1, (j - 1) % TOPK, first and j < 3)
                    if j % 2 == 1 and not (first and j == 1):
                        x2_out(g * BG + (j - 3) // 2, ((j - 3) // 2) % 2)
                    if not first:
                        if j == 2:
                            l2_lo_part(g - 1)
                        elif j == 5:
                            l2_scale(g - 1, l2_first)
                        elif j == 7:
                            x3_out(g - 1)

            dve.wait_ge(route_ready, 1)
            dve.wait_ge(skill_in, 16 * N_SKILL)
            copy_gu(0, 0, True)
            shared_lo(NG * NC - 1, 1, False)
            shared_y(NG - 1)
            dve.wait_ge(sh_y_done, NG)
            dve.wait_ge(setup_dve, 1)
            expert_group(0, True)
            expert_group(1, False, l2_first=True)
            with dve.Fori(2, NG) as g:
                expert_group(g, False)

            def copy_w3(b, j, first):
                if not first:
                    dve.wait_ge(dn3_done, b - BG + 1)
                e = dve.value_load(best_e[0:1, bass.ds(b, 1)], min_val=0, max_val=E - 1)
                dve.tensor_copy(batch_w3[:, j, :], w3[:, bass.ds(e, 1), :].rearrange("p a n -> p (a n)")
                                ).then_inc(w3_copied, 1)

            def hidden3(b, j, first):
                dve.wait_ge(gate3_done, b + 1)
                dve.wait_ge(b3_copied, b + 1)
                if not first:
                    dve.wait_ge(dn3_done, b - 1)
                for c in range(NC3):
                    cs = slice(c * S, (c + 1) * S)
                    dve.wait_ge(silu_done, b * NC3 + c + 1)
                    dve.scalar_tensor_tensor(out=hid3[:, j % 2, cs], in0=gu[:, 2 + j % 2, cs],
                                             scalar=batch_b3[:, j, NC3 + c:NC3 + c + 1], in1=silu_s[:, j % 2, cs],
                                             op0=ALU.add, op1=ALU.mult).then_inc(hid3_done, 1)

            def out3(b, j):
                c = bass.ds(b * S, S)
                dve.wait_ge(dn3_done, b + 1)
                dve.scalar_tensor_tensor(out=x3T[:, c], in0=yy[:, j % 2, 0:S], scalar=batch_b3[:, j, 2 * NC3:],
                                         in1=x3T[:, c], op0=ALU.add, op1=ALU.add).then_inc(out_done, 1)

            def l3_group(g, first):
                for j in range(BG):
                    b = g * BG + j
                    copy_w3(b, j, first)
                    if first and j == 0:
                        x2_out(B - 1, (B - 1) % 2)
                        l2_lo_part(NG - 1)
                    else:
                        hidden3(b - 1, (j - 1) % BG, first and j < 3)
                    if not (first and j < 2):
                        out3(b - 2, (j - 2) % BG)
                    if first and j == 2:
                        l2_scale(NG - 1, False)
                    if first and j == 3:
                        x3_out(NG - 1)

            dve.wait_ge(w3_in, 16 * N_W3)
            expert_prod(NP - 1, TOPK - 1, False)
            l3_group(0, True)
            with dve.Fori(1, NG) as g:
                l3_group(g, False)
            hidden3(B - 1, BG - 1, False)
            out3(B - 2, BG - 2)
            out3(B - 1, BG - 1)


def kernel(x, cond_8, L0_cond_weight, L0_cond_mask, L0_cond_bias, L1_cond_skill_gate, L1_cond_skill_up,
           L1_cond_skill_down, L1_cond_shared_gate, L1_cond_shared_up, L1_cond_shared_down, L2_cond_W_base,
           L2_cond_b_base, L2_cond_As, L2_cond_Bs, L3_cond_W_up, L3_cond_b_up, L3_cond_W_gate, L3_cond_b_gate,
           L3_cond_W_down, L3_cond_b_down):
    import numpy as np
    import concourse.bacc as bacc
    from concourse.bass_utils import run_bass_kernel_spmd

    B, S, D = x.shape
    E = cond_8.shape[1]
    OI = D // E
    H3 = L3_cond_W_up.shape[1]

    def lay(a, *axes):
        a = np.asarray(a)
        return np.ascontiguousarray(a.transpose(*axes) if axes else a)

    def by_partition(b):
        b = np.asarray(b)
        return np.ascontiguousarray(b.reshape(E, -1, D).transpose(2, 0, 1))

    ins = {
        "xT": lay(x, 2, 0, 1).reshape(D, B * S),
        "cond": lay(cond_8),
        "condT": lay(cond_8, 1, 0),
        "w0": lay(np.asarray(L0_cond_weight).reshape(E, D // OI, OI, D), 0, 2, 1, 3).reshape(D, -1),
        "mask": lay(np.asarray(L0_cond_mask).reshape(D // OI, OI, D), 1, 0, 2).reshape(OI, -1),
        "bias0": lay(L0_cond_bias).reshape(D, 1),
        "sk_gate": lay(L1_cond_skill_gate),
        "sk_up": lay(L1_cond_skill_up),
        "sk_down": lay(L1_cond_skill_down),
        "sh_gate": lay(L1_cond_shared_gate),
        "sh_up": lay(L1_cond_shared_up),
        "sh_down": lay(L1_cond_shared_down),
        "wbase": lay(L2_cond_W_base, 1, 0),
        "bbase": lay(L2_cond_b_base).reshape(D, 1),
        "lora_a": lay(L2_cond_As, 2, 0, 1).reshape(D, -1),
        "lora_b": lay(L2_cond_Bs, 0, 2, 1).reshape(D, -1),
        "w3": np.concatenate([
            lay(L3_cond_W_up, 2, 0, 1), lay(L3_cond_W_gate, 2, 0, 1),
            lay(np.asarray(L3_cond_W_down).reshape(E, D, H3 // D, D), 3, 0, 2, 1).reshape(D, E, H3)], axis=2),
        "b3": np.concatenate([by_partition(b) for b in (L3_cond_b_up, L3_cond_b_gate, L3_cond_b_down)], axis=2),
    }
    nc = bacc.Bacc("TRN2", target_bir_lowering=False, num_devices=1)
    aps = [nc.dram_tensor(n + "_dram", a.shape, mybir.dt.from_np(a.dtype), kind="ExternalInput").ap() for n, a in ins.items()]
    out = nc.dram_tensor("outT_dram", (D, B * S), F32, kind="ExternalOutput").ap()
    cond_resid_kernel(nc, *aps, out)
    r = run_bass_kernel_spmd(nc, [{n + "_dram": a for n, a in ins.items()}], core_ids=[0])
    got = r.results[0]["outT_dram"]
    return np.ascontiguousarray(got.reshape(D, B, S).transpose(1, 2, 0))
```

```python
from contextlib import ExitStack

import concourse.bass as bass
from concourse import mybir

F32 = mybir.dt.float32
F32R = mybir.dt.float32r
I32 = mybir.dt.int32
ALU = mybir.AluOpType
ACT = mybir.ActivationFunctionType
AX = mybir.AxisListType

P = 128


def cond_resid_kernel(
    nc, xT_d, cond_d, condT_d, w0_d, mask_d, bias0_d,
    sk_gate_d, sk_up_d, sk_down_d, sh_gate_d, sh_up_d, sh_down_d,
    wbase_d, bbase_d, lora_a_d, lora_b_d,
    w3_d, b3_d, outT_d,
):
    TOK = xT_d.shape[1]
    B, E = cond_d.shape
    S = TOK // B
    I = sh_gate_d.shape[1]
    NC = I // P
    H3 = w3_d.shape[2] // 3
    NC3 = H3 // P
    GT = 512
    NG = TOK // GT
    BG = GT // S
    TOPK = 2
    PG = BG * TOPK
    NP = B * TOPK
    OI = P // E
    OB = P // OI
    WARM = 20
    LORA_SCALE = 2.0
    MOE_SCALE = 1.0 / 12
    W3 = 3 * H3
    NB3 = 2 * NC3 + 1
    assert S == P and B * E == P and NG == 4 and NC == 4 and NC3 == 2 and BG == 4

    with ExitStack() as ctx:
        def sb(name, shape, dt=F32):
            return ctx.enter_context(nc.sbuf_tensor(name, shape, dt))

        def sem(name):
            return ctx.enter_context(nc.semaphore(name))

        xT = sb("xT", [P, TOK])
        x_hi = sb("x_hi", [P, TOK], F32R)
        x_lo = sb("x_lo", [P, TOK], F32R)
        yT = sb("yT", [P, TOK])
        x3T = sb("x3T", [P, TOK])
        w0 = sb("w0", [P, OB * P])
        mask = sb("mask", [P, OB * P])
        cond_rep = sb("cond_rep", [P, B])
        cond_rep2 = sb("cond_rep2", [P, B])
        delta16 = sb("delta16", [P, OI])
        y_kron = sb("y_kron", [P, B, OI])
        wbotT = sb("wbotT", [P, B, P])
        ident = sb("ident", [P, P])
        spare = sb("spare", [P, 1])
        biases = sb("biases", [P, 2])
        cond_bc = sb("cond_bc", [P, B, E])
        rev = sb("rev", [P, E])
        rev_i = sb("rev_i", [P, E], I32)
        r_a = sb("r_a", [P, B, E])
        r_b = sb("r_b", [P, B, E])
        r_w = sb("r_w", [P, B, E])
        r_w2 = sb("r_w2", [P, B, E])
        r_s = sb("r_s", [P, 8, B])
        pair_w0 = sb("pair_w0", [P, B, TOPK])
        pair_w1 = sb("pair_w1", [P, B, TOPK])
        pair_w = sb("pair_w", [P, B, TOPK])
        pair_e = sb("pair_e", [P, B, TOPK], I32)
        best_e = sb("best_e", [P, B], I32)
        sh_raw = sb("sh_raw", [P, 3, I])
        sh_hi = sb("sh_hi", [P, 3, I], F32R)
        sh_lo = sb("sh_lo", [P, 3, I], F32R)
        gelu_s = sb("gelu_s", [P, 2, GT])
        prod_s = sb("prod_s", [P, 2, GT])
        prod_hi = sb("prod_hi", [P, 2, GT], F32R)
        prod_lo = sb("prod_lo", [P, 2, GT], F32R)
        sk_gu = sb("sk_gu", [P, E, 2 * I])
        sk_dn = sb("sk_dn", [P, E, I])
        pair_gu_buf = sb("pair_gu", [P, 2, 2 * I])
        pair_dn = sb("pair_dn", [P, 2, I])
        wbot_place = wbotT[:].rearrange("p b o -> p (b o)")
        pair_gu = [pair_gu_buf[:, 0, :], pair_gu_buf[:, 1, :], wbot_place[:, 0:2 * I], wbot_place[:, 2 * I:4 * I]]
        l2_raw = sb("l2_raw", [P, 3, P])
        l2_hi = sb("l2_hi", [P, 2, P], F32R)
        l2_lo = sb("l2_lo", [P, 2, P], F32R)
        lora_h = sb("lora_h", [P, BG, S])
        w3 = sb("w3", [P, E, W3])
        b3 = sb("b3", [P, E, NB3])
        batch_w3 = sb("batch_w3", [P, BG, W3])
        batch_b3 = sb("batch_b3", [P, B, NB3])
        silu_s = sb("silu_s", [P, 2, H3])
        hid3 = sb("hid3", [P, BG, H3])

        gu = ctx.enter_context(nc.psum_tensor("gu", [P, 4, GT], F32))
        yy = ctx.enter_context(nc.psum_tensor("yy", [P, 4, GT], F32))

        cond_in, w0_in, mask_in, x_in = sem("cond_in"), sem("w0_in"), sem("mask_in"), sem("x_in")
        shgu_in, shdn_in, l2_in, skill_in, w3_in = (
            sem("shgu_in"), sem("shdn_in"), sem("l2_in"), sem("skill_in"), sem("w3_in"))
        out_stored = sem("out_stored")
        pool_const = sem("pool_const")
        route_step = sem("route_step")
        exp_ready, exp_in_ready, route_ready = sem("exp_ready"), sem("exp_in_ready"), sem("route_ready")
        setup_dve = sem("setup_dve")
        kron_ready, masked_ready = sem("kron_ready"), sem("masked_ready")
        wbot_done, wbot_act, wbot_dve = sem("wbot_done"), sem("wbot_act"), sem("wbot_dve")
        l0_done, x1_done, x1hi_done, x1lo_dve, x1lo_pool = (
            sem("l0_done"), sem("x1_done"), sem("x1hi_done"), sem("x1lo_dve"), sem("x1lo_pool"))
        whi_done, wlo_done = sem("whi_done"), sem("wlo_done")
        sh_g_done, sh_u_done, sh_dn_done = sem("sh_g_done"), sem("sh_u_done"), sem("sh_dn_done")
        sh_gelu_done, sh_prod_done, sh_hi_done, sh_lo_done, sh_y_done = (
            sem("sh_gelu_done"), sem("sh_prod_done"), sem("sh_hi_done"), sem("sh_lo_done"), sem("sh_y_done"))
        gu0_copied = sem("gu0_copied")
        gu_copied, dn_copied = sem("gu_copied"), sem("dn_copied")
        ex_g_done, ex_u_done, ex_dn_done = sem("ex_g_done"), sem("ex_u_done"), sem("ex_dn_done")
        ex_gelu_done, ex_prod_done, x2_done = sem("ex_gelu_done"), sem("ex_prod_done"), sem("x2_done")
        l2_hi_done, l2_lo_done, l2_h_done, l2_hs_done, l2_x_done, x3_done = (
            sem("l2_hi_done"), sem("l2_lo_done"), sem("l2_h_done"), sem("l2_hs_done"), sem("l2_x_done"), sem("x3_done"))
        w3_copied, dn3_copied, b3_copied = sem("w3_copied"), sem("dn3_copied"), sem("b3_copied")
        up3_done, gate3_done, dn3_done = sem("up3_done"), sem("gate3_done"), sem("dn3_done")
        silu_done, hid3_done, out_done = sem("silu_done"), sem("hid3_done"), sem("out_done")

        assert wbot_place.shape[1] == 4 * I
        N_SKILL = 3 * E
        N_W3 = 2

        def cols(i, n):
            return bass.ds(i * n, n)

        bias3 = batch_b3[:].rearrange("p b n -> p (b n)")
        pair_w_cols = pair_w[:].rearrange("p b k -> p (b k)")
        pair_e_cols = pair_e[:].rearrange("p b k -> p (b k)")
        xT_b = xT[:]
        block = ctx.enter_context(nc.Block())

        @block.sync
        def _(sp):
            sp.dma_start(cond_rep[:], bass.AP(condT_d.tensor, 0, [[B, E], [0, OI], [1, B]])).then_inc(cond_in, 16)
            sp.dma_start(w0[:], w0_d).then_inc(w0_in, 16)
            for g in range(NG):
                sp.dma_start(xT[:, g * GT:(g + 1) * GT], xT_d[:, g * GT:(g + 1) * GT]).then_inc(x_in, 16)
            sp.dma_start(sh_raw[:, 0, :], sh_gate_d).then_inc(shgu_in, 16)
            sp.dma_start(sh_raw[:, 1, :], sh_up_d).then_inc(shgu_in, 16)
            sp.dma_start(sh_raw[:, 2, :].rearrange("p (c h) -> p c h", c=NC),
                         sh_down_d.rearrange("(c p) h -> p c h", p=P)).then_inc(shdn_in, 16)
            sp.dma_start(l2_raw[:, 0, :], wbase_d).then_inc(l2_in, 16)
            sp.dma_start(l2_raw[:, 1, :], lora_a_d).then_inc(l2_in, 16)
            sp.dma_start(l2_raw[:, 2, :], lora_b_d).then_inc(l2_in, 16)
            for e in range(E):
                sp.dma_start(sk_gu[:, e, 0:I], sk_gate_d[e]).then_inc(skill_in, 16)
                sp.dma_start(sk_gu[:, e, I:2 * I], sk_up_d[e]).then_inc(skill_in, 16)
                sp.dma_start(sk_dn[:, e, :].rearrange("p (c h) -> p c h", c=NC),
                             sk_down_d[e].rearrange("(c p) h -> p c h", p=P)).then_inc(skill_in, 16)
            sp.dma_start(w3[:], w3_d).then_inc(w3_in, 16)
            sp.dma_start(b3[:], b3_d).then_inc(w3_in, 16)
            for g in range(NG):
                sp.wait_ge(out_done, (g + 1) * BG)
                sp.dma_start(outT_d[:, g * GT:(g + 1) * GT], x3T[:, g * GT:(g + 1) * GT]).then_inc(out_stored, 16)
            sp.wait_ge(out_stored, 16 * NG)

        @block.gpsimd
        def _(pool):
            pool.memset(ident[:], 0.0).then_inc(pool_const, 1)
            pool.iota(rev_i[:], [[-1, E]], base=E, channel_multiplier=0).then_inc(pool_const, 1)
            pool.wait_ge(pool_const, 2)
            pool.affine_select(out=ident[:], in_=ident[:], compare_op=ALU.not_equal, fill=1.0, base=0,
                               pattern=[[-1, P]], channel_multiplier=1).then_inc(pool_const, 1)
            for g in range(1, NG):
                c = slice(g * GT, (g + 1) * GT)
                pool.wait_ge(x1hi_done, g + 1)
                pool.tensor_tensor(x_lo[:, c], xT[:, c], x_hi[:, c].bitcast(F32), ALU.subtract).then_inc(x1lo_pool, 1)
            pool.wait_ge(route_ready, 1)
            pool.wait_ge(skill_in, 16 * N_SKILL)
            e = pool.value_load(pair_e_cols[0:1, 0:1], min_val=0, max_val=E - 1)
            pool.tensor_copy(pair_gu[0], sk_gu[:, bass.ds(e, 1), :].rearrange("p a n -> p (a n)")
                             ).then_inc(gu0_copied, 1)
            pool.wait_ge(w3_in, 16 * N_W3)
            with pool.Fori(0, B) as b:
                e = pool.value_load(best_e[0:1, bass.ds(b, 1)], min_val=0, max_val=E - 1)
                pool.tensor_copy(batch_b3[:, bass.ds(b, 1), :].rearrange("p a n -> p (a n)"),
                                 b3[:, bass.ds(e, 1), :].rearrange("p a n -> p (a n)")).then_inc(b3_copied, 1)

        @block.tensor
        def _(pe):
            def split3(out, w_hi, w_lo, m_hi, m_lo, start, stop):
                pe.matmul(out, w_hi, m_hi, start=start, stop=False)
                pe.matmul(out, w_hi, m_lo, start=False, stop=False)
                return pe.matmul(out, w_lo, m_hi, start=False, stop=stop)

            pe.wait_ge(pool_const, 3)
            for _ in range(WARM):
                pe.matmul(yy[:, 0, 0:P], ident[:], ident[:], start=True, stop=True)
            pe.wait_ge(kron_ready, 1)
            pe.wait_ge(masked_ready, 1)
            for ob in range(OB):
                pe.matmul(gu[:, ob // 2, (ob % 2) * B * OI:(ob % 2 + 1) * B * OI], w0[:, ob * P:(ob + 1) * P],
                          y_kron[:].rearrange("p b o -> p (b o)"), start=True, stop=True).then_inc(wbot_done, 1)
            pe.wait_ge(wbot_act, 2)
            pe.wait_ge(wbot_dve, 2)
            for g in range(NG):
                pe.wait_ge(x_in, 16 * NG)
                for b in range(g * BG, (g + 1) * BG):
                    mm = pe.matmul(yy[:, g, (b % BG) * S:(b % BG + 1) * S], wbotT[:, b, :], xT[:, b * S:(b + 1) * S],
                                   start=True, stop=True)
                mm.then_inc(l0_done, 1)

            def shared_up(g, c, first):
                q = g * NC + c
                tok = bass.ds(g * GT, GT)
                ch = slice(c * P, (c + 1) * P)
                if not (first and c < 2):
                    pe.wait_ge(sh_gelu_done, q - 1)
                split3(gu[:, c % 2, :], sh_hi[:, 0, ch], sh_lo[:, 0, ch], x_hi[:, tok], x_lo[:, tok],
                       True, True).then_inc(sh_g_done, 1)
                if not (first and c < 2):
                    pe.wait_ge(sh_prod_done, q - 1)
                split3(gu[:, 2 + c % 2, :], sh_hi[:, 1, ch], sh_lo[:, 1, ch], x_hi[:, tok], x_lo[:, tok],
                       True, True).then_inc(sh_u_done, 1)

            def shared_down(g, c):
                q = g * NC + c
                ch = slice(c * P, (c + 1) * P)
                pe.wait_ge(sh_hi_done, q + 1)
                pe.wait_ge(sh_lo_done, q + 1)
                out = yy[:, bass.ds(g, 1), :].rearrange("p a n -> p (a n)")
                split3(out, sh_hi[:, 2, ch], sh_lo[:, 2, ch], prod_hi[:, c % 2, :], prod_lo[:, c % 2, :],
                       c == 0, c == NC - 1).then_inc(sh_dn_done, 1)

            def shared_group(g, first):
                pe.wait_ge(x1hi_done, g + 1)
                if first:
                    pe.wait_ge(x1lo_dve, 1)
                else:
                    pe.wait_ge(x1lo_pool, g)
                for c in range(NC):
                    shared_up(g, c, first)
                    if c >= 2:
                        shared_down(g, c - 2)
                    elif not first:
                        shared_down(g - 1, c + NC - 2)

            pe.wait_ge(whi_done, 2)
            pe.wait_ge(wlo_done, 2)
            shared_group(0, True)
            with pe.Fori(1, NG) as g:
                shared_group(g, False)

            def expert_up(b, k, par, first):
                p = b * TOPK + k
                w = pair_gu[par % len(pair_gu)]
                if first and par == 0:
                    pe.wait_ge(gu0_copied, 1)
                else:
                    pe.wait_ge(gu_copied, p)
                tok = bass.ds(b * S, S)
                if first and par < 2:
                    pe.wait_ge(sh_gelu_done, NG * NC - 1 + par)
                else:
                    pe.wait_ge(ex_gelu_done, p - 1)
                for c in range(NC):
                    mm = pe.matmul(gu[:, k, c * S:(c + 1) * S], w[:, c * P:(c + 1) * P], xT[:, tok],
                                   start=True, stop=True)
                mm.then_inc(ex_g_done, 1)
                if first and par < 2:
                    pe.wait_ge(sh_prod_done, NG * NC - 1 + par)
                else:
                    pe.wait_ge(ex_prod_done, p - 1)
                for c in range(NC):
                    mm = pe.matmul(gu[:, 2 + k, c * S:(c + 1) * S], w[:, I + c * P:I + (c + 1) * P],
                                   xT[:, tok], start=True, stop=True)
                mm.then_inc(ex_u_done, 1)

            def expert_down(b, k, ypar, first):
                p = b * TOPK + k
                pe.wait_ge(ex_prod_done, p + 1)
                pe.wait_ge(dn_copied, p + 1)
                if k == 0:
                    if first:
                        pe.wait_ge(sh_y_done, ypar + 1)
                    else:
                        pe.wait_ge(x2_done, b - 1)
                for c in range(NC):
                    mm = pe.matmul(yy[:, ypar, 0:S], pair_dn[:, k, c * P:(c + 1) * P],
                                   prod_s[:, k, c * S:(c + 1) * S],
                                   start=(k == 0 and c == 0), stop=(k == TOPK - 1 and c == NC - 1))
                mm.then_inc(ex_dn_done, 1)

            def lora_in(g):
                tok = bass.ds(g * GT, GT)
                pe.wait_ge(l2_hi_done, g + 1)
                pe.wait_ge(l2_lo_done, g + 1)
                split3(yy[:, 2, :], l2_hi[:, 1, :], l2_lo[:, 1, :], x_hi[:, tok], x_lo[:, tok],
                       True, True).then_inc(l2_h_done, 1)
                split3(yy[:, 3, :], l2_hi[:, 0, :], l2_lo[:, 0, :], x_hi[:, tok], x_lo[:, tok], True, False)

            def lora_out(g):
                pe.wait_ge(l2_hs_done, g + 1)
                pe.matmul(yy[:, 3, :], l2_raw[:, 2, :], lora_h[:].rearrange("p b s -> p (b s)"),
                          start=False, stop=True).then_inc(l2_x_done, 1)

            def expert_group(g, first):
                for j in range(PG):
                    b, k = g * BG + j // TOPK, j % TOPK
                    if not (first and j == 0):
                        expert_up(b, k, j, first)
                    if j >= 1:
                        jb, jk = (j - 1) // TOPK, (j - 1) % TOPK
                        expert_down(g * BG + jb, jk, jb % 2, first and jb < 2)
                    elif not first:
                        expert_down(g * BG - 1, TOPK - 1, (BG - 1) % 2, False)
                    if not first and j == 4:
                        lora_in(g - 1)
                    if not first and j == 6:
                        lora_out(g - 1)

            shared_down(NG - 1, NC - 2)
            expert_up(0, 0, 0, True)
            shared_down(NG - 1, NC - 1)
            expert_group(0, True)
            pe.wait_ge(whi_done, 4)
            pe.wait_ge(wlo_done, 4)
            pe.wait_ge(sh_y_done, NG)
            with pe.Fori(1, NG) as g:
                expert_group(g, False)

            def up3(b, j, first):
                tok = bass.ds(b * S, S)
                pe.wait_ge(w3_copied, b + 1)
                if first and j < 2:
                    pe.wait_ge(ex_gelu_done, NP - 1 + j)
                    pe.wait_ge(x3_done, 1)
                else:
                    pe.wait_ge(silu_done, (b - 1) * NC3)
                for c in range(NC3):
                    mm = pe.matmul(gu[:, j % 2, c * S:(c + 1) * S], batch_w3[:, j, c * P:(c + 1) * P], xT3(tok),
                                   start=True, stop=True)
                mm.then_inc(up3_done, 1)
                if first and j < 2:
                    pe.wait_ge(ex_prod_done, NP - 1 + j)
                else:
                    pe.wait_ge(hid3_done, (b - 1) * NC3)
                for c in range(NC3):
                    mm = pe.matmul(gu[:, 2 + j % 2, c * S:(c + 1) * S], batch_w3[:, j, H3 + c * P:H3 + (c + 1) * P],
                                   xT3(tok), start=True, stop=True)
                mm.then_inc(gate3_done, 1)

            def xT3(tok):
                return x3T[:, tok]

            def down3(b, j, first):
                if first and j < 2:
                    pe.wait_ge(x2_done, B - 1 + j)
                else:
                    pe.wait_ge(out_done, b - 1)
                pe.wait_ge(dn3_copied, b + 1)
                for c in range(NC3):
                    pe.wait_ge(hid3_done, b * NC3 + c + 1)
                    mm = pe.matmul(yy[:, j % 2, 0:S], batch_w3[:, j, 2 * H3 + c * P:2 * H3 + (c + 1) * P],
                                   hid3[:, j, c * S:(c + 1) * S], start=(c == 0), stop=(c == NC3 - 1))
                mm.then_inc(dn3_done, 1)

            def l3_group(g, first):
                if not first:
                    pe.wait_ge(x3_done, g + 1)
                for j in range(BG):
                    b = g * BG + j
                    up3(b, j, first)
                    if first and j == 0:
                        expert_down(B - 1, TOPK - 1, (B - 1) % 2, False)
                    if not (first and j < 2):
                        down3(b - 2, (j - 2) % BG, first)
                    if first and j == 2:
                        lora_in(NG - 1)
                    if first and j == 3:
                        lora_out(NG - 1)

            l3_group(0, True)
            with pe.Fori(1, NG) as g:
                l3_group(g, False)
            down3(B - 2, BG - 2, False)
            down3(B - 1, BG - 1, False)

        @block.scalar
        def _(act):
            act.dma_start(cond_bc[:].rearrange("p b e -> p (b e)"),
                          bass.AP(cond_d.tensor, 0, [[0, P], [1, B * E]])).then_inc(cond_in, 16)
            act.dma_start(mask[:], bass.AP(mask_d.tensor, 0, [[0, E], [OB * P, OI], [1, OB * P]])).then_inc(mask_in, 16)
            act.dma_start(biases[:, 0:1], bias0_d).then_inc(l2_in, 16)
            act.dma_start(biases[:, 1:2], bbase_d).then_inc(l2_in, 16)
            act.wait_ge(exp_in_ready, 1)
            act.activation(r_b[:], r_a[:], ACT.Exp).then_inc(exp_ready, 1)
            act.wait_ge(pool_const, 3)
            act.activation(spare[:], ident[:, 0:1], ACT.Gelu_apprx_tanh)
            def wbot_out(k):
                act.wait_ge(wbot_done, 2 * k + 2)
                act.activation(wbotT[:, :, 2 * k * OI:(2 * k + 2) * OI].rearrange("p b (a o) -> p a b o", a=2),
                               gu[:, k, :].rearrange("p (a b o) -> p a b o", a=2, b=B), ACT.Copy).then_inc(wbot_act, 1)

            wbot_out(0)
            act.wait_ge(shgu_in, 32)
            act.activation(sh_hi[:, 0, :], sh_raw[:, 0, :], ACT.Copy).then_inc(whi_done, 1)
            wbot_out(2)
            act.activation(sh_hi[:, 1, :], sh_raw[:, 1, :], ACT.Copy).then_inc(whi_done, 1)

            def x1_hi(g):
                c = slice(g * GT, (g + 1) * GT)
                act.wait_ge(x1_done, g + 1)
                act.activation(x_hi[:, c], xT[:, c], ACT.Copy).then_inc(x1hi_done, 1)

            x1_hi(0)
            act.wait_ge(shdn_in, 16)
            act.activation(sh_hi[:, 2, :], sh_raw[:, 2, :], ACT.Copy).then_inc(whi_done, 1)
            x1_hi(1)

            def shared_gelu(q, par, first):
                act.wait_ge(sh_g_done, q + 1)
                if not first:
                    act.wait_ge(sh_prod_done, q - 1)
                act.activation(gelu_s[:, par, :], gu[:, par, :], ACT.Gelu_apprx_tanh).then_inc(sh_gelu_done, 1)

            def shared_hi(q, par, first):
                act.wait_ge(sh_prod_done, q + 1)
                if not first:
                    act.wait_ge(sh_dn_done, q - 1)
                act.activation(prod_hi[:, par, :], prod_s[:, par, :], ACT.Copy).then_inc(sh_hi_done, 1)

            def shared_group(g, first):
                for c in range(NC):
                    shared_gelu(g * NC + c, c % 2, first and c < 2)
                    if not (first and c == 0):
                        shared_hi(g * NC + c - 1, (c - 1) % 2, first and c < 3)
                    if first and 1 <= c <= 2:
                        x1_hi(c + 1)

            shared_group(0, True)
            act.wait_ge(l2_in, 16 * 5)
            act.activation(l2_hi[:], l2_raw[:, 0:2, :], ACT.Copy).then_inc(whi_done, 1)
            with act.Fori(1, NG) as g:
                shared_group(g, False)

            def pair_expert(p):
                return act.value_load(pair_e_cols[0:1, bass.ds(p, 1)], min_val=0, max_val=E - 1)

            def copy_down(p, k, e, first):
                if not first:
                    act.wait_ge(ex_dn_done, p - 1)
                act.activation(pair_dn[:, k, :], sk_dn[:, bass.ds(e, 1), :].rearrange("p a n -> p (a n)"),
                               ACT.Copy).then_inc(dn_copied, 1)

            def expert_gelu(p, k, first):
                act.wait_ge(ex_g_done, p + 1)
                if not first:
                    act.wait_ge(ex_prod_done, p - 1)
                act.activation(gelu_s[:, k, :], gu[:, k, :], ACT.Gelu_apprx_tanh).then_inc(ex_gelu_done, 1)

            def l2_split(g):
                c = bass.ds(g * GT, GT)
                act.wait_ge(x2_done, (g + 1) * BG)
                act.activation(x_hi[:, c], yT[:, c], ACT.Copy).then_inc(l2_hi_done, 1)

            def expert_group(g, first):
                for j in range(PG):
                    if not (first and j == 0):
                        expert_gelu(g * PG + j - 1, (j - 1) % TOPK, first and j < 3)
                        if j == first:
                            e = pair_expert(g * PG + j)
                        copy_down(g * PG + j, j % TOPK, e, first and j < 2)
                        if j < PG - 1:
                            e = pair_expert(g * PG + j + 1)
                    if not first and j == 2:
                        l2_split(g - 1)

            act.wait_ge(route_ready, 1)
            act.wait_ge(skill_in, 16 * N_SKILL)
            copy_down(0, 0, pair_expert(0), True)
            shared_hi(NG * NC - 1, 1, False)
            expert_group(0, True)
            with act.Fori(1, NG) as g:
                expert_group(g, False)

            def batch_expert(b):
                return act.value_load(best_e[0:1, bass.ds(b, 1)], min_val=0, max_val=E - 1)

            def copy_dn3(b, j, e, first):
                if not first:
                    act.wait_ge(dn3_done, b - BG + 1)
                act.activation(batch_w3[:, j, 2 * H3:], w3[:, bass.ds(e, 1), 2 * H3:].rearrange("p a n -> p (a n)"),
                               ACT.Copy).then_inc(dn3_copied, 1)

            def silu3(b, j, first):
                act.wait_ge(up3_done, b + 1)
                if not first:
                    act.wait_ge(hid3_done, (b - 1) * NC3)
                for c in range(NC3):
                    cs = slice(c * S, (c + 1) * S)
                    act.activation(silu_s[:, j % 2, cs], gu[:, j % 2, cs], ACT.Silu,
                                   bias=bias3[:, bass.ds(b * NB3 + c, 1)]).then_inc(silu_done, 1)

            def l3_group(g, first=False, last=False):
                for j in range(BG):
                    b = g * BG + j
                    if not (first and j == 0):
                        silu3(b - 1, (j - 1) % BG, first and j < 3)
                    else:
                        l2_split(NG - 1)
                    if j == 0:
                        e = batch_expert(b + 1)
                    if not (last and j == BG - 1):
                        copy_dn3(b + 1, (j + 1) % BG, e, first and j < BG - 1)
                    if j < BG - 2 + (not last):
                        e = batch_expert(b + 2)

            act.wait_ge(w3_in, 16 * N_W3)
            expert_gelu(NP - 1, TOPK - 1, False)
            act.activation(spare[:], ident[:, 0:1], ACT.Silu)
            copy_dn3(0, 0, batch_expert(0), True)
            act.wait_ge(b3_copied, B)
            l3_group(0, first=True)
            with act.Fori(1, NG - 1) as g:
                l3_group(g)
            l3_group(NG - 1, last=True)
            silu3(B - 1, BG - 1, False)

        @block.vector
        def _(dve):
            step = [0]

            def link(ins):
                step[0] += 1
                ins.then_inc(route_step, 1)
                dve.wait_ge(route_step, step[0])

            def over_e(a):
                return a.rearrange("p (b o) -> p b o", o=1).broadcast_to([P, B, E])

            def over_b(a):
                return a.rearrange("p (o e) -> p o e", o=1).broadcast_to([P, B, E])

            cmax, esum, rsum, best, bestr, sec, secr, topr = (r_s[:, i, :] for i in range(8))

            def top_expert():
                link(dve.tensor_tensor(r_w2[:], cond_bc[:], over_e(cmax), ALU.is_equal))
                link(dve.tensor_tensor(r_w2[:], r_w2[:], over_b(rev[:]), ALU.mult))
                link(dve.tensor_reduce(topr, r_w2[:], AX.X, ALU.max))
                link(dve.tensor_scalar(best_e[:], topr, -1.0, float(E), ALU.mult, ALU.add))

            def softmax():
                dve.wait_ge(exp_ready, 1)
                link(dve.tensor_reduce(esum, r_b[:], AX.X, ALU.add))
                link(dve.reciprocal(rsum, esum))
                link(dve.tensor_tensor(r_w[:], r_b[:], over_e(rsum), ALU.mult))

            def best_expert():
                link(dve.tensor_reduce(best, r_w[:], AX.X, ALU.max))
                link(dve.tensor_tensor(r_a[:], r_w[:], over_e(best), ALU.is_equal))
                link(dve.tensor_tensor(r_a[:], r_a[:], over_b(rev[:]), ALU.mult))
                link(dve.tensor_reduce(bestr, r_a[:], AX.X, ALU.max))

            def second_value():
                link(dve.tensor_tensor(r_a[:], over_b(rev[:]), over_e(bestr), ALU.is_equal))
                link(dve.scalar_tensor_tensor(out=r_w2[:], in0=r_a[:], scalar=-2.0, in1=r_w[:],
                                              op0=ALU.mult, op1=ALU.add))
                link(dve.tensor_reduce(sec, r_w2[:], AX.X, ALU.max))

            def second_expert():
                link(dve.tensor_tensor(r_a[:], r_w2[:], over_e(sec), ALU.is_equal))
                link(dve.tensor_tensor(r_a[:], r_a[:], over_b(rev[:]), ALU.mult))
                link(dve.tensor_reduce(secr, r_a[:], AX.X, ALU.max))

            def pair_indices():
                link(dve.tensor_scalar(pair_e[:, :, 0], bestr, -1.0, float(E), ALU.mult, ALU.add))
                link(dve.tensor_scalar(pair_e[:, :, 1], secr, -1.0, float(E), ALU.mult, ALU.add))
                link(dve.tensor_tensor(esum, best, sec, ALU.add))
                link(dve.reciprocal(rsum, esum))

            def pair_weights():
                link(dve.tensor_tensor(pair_w0[:, :, 0], best, rsum, ALU.mult))
                link(dve.tensor_tensor(pair_w0[:, :, 1], sec, rsum, ALU.mult))
                link(dve.tensor_scalar(pair_w1[:], pair_w0[:], 1.0 - MOE_SCALE, None, ALU.mult))
                dve.scalar_tensor_tensor(out=pair_w[:], in0=pair_w0[:], scalar=MOE_SCALE, in1=pair_w1[:],
                                         op0=ALU.mult, op1=ALU.add).then_inc(route_ready, 1)

            dve.wait_ge(pool_const, 3)
            dve.tensor_reduce(delta16[:], ident[:].rearrange("p (k o) -> p o k", o=OI), AX.X,
                              ALU.add).then_inc(setup_dve, 1)
            dve.wait_ge(setup_dve, 1)
            dve.wait_ge(cond_in, 32)
            dve.tensor_tensor(y_kron[:], cond_rep[:].rearrange("p (b o) -> p b o", o=1).broadcast_to([P, B, OI]),
                              delta16[:].rearrange("p (b o) -> p b o", b=1).broadcast_to([P, B, OI]),
                              ALU.mult).then_inc(kron_ready, 1)
            link(dve.tensor_copy(rev[:], rev_i[:]))
            link(dve.tensor_reduce(cmax, cond_bc[:], AX.X, ALU.max))
            dve.tensor_tensor(r_a[:], cond_bc[:], over_e(cmax), ALU.subtract).then_inc(exp_in_ready, 1)
            top_expert()
            dve.wait_ge(w0_in, 16)
            dve.wait_ge(mask_in, 16)
            dve.tensor_tensor(w0[:], w0[:], mask[:], ALU.mult).then_inc(masked_ready, 1)
            dve.tensor_scalar(cond_rep2[:], cond_rep[:], LORA_SCALE, None, ALU.mult).then_inc(setup_dve, 1)
            def wbot_out(k):
                dve.wait_ge(wbot_done, 2 * k + 2)
                dve.tensor_copy(wbotT[:, :, 2 * k * OI:(2 * k + 2) * OI].rearrange("p b (a o) -> p a b o", a=2),
                                gu[:, k, :].rearrange("p (a b o) -> p a b o", a=2, b=B)).then_inc(wbot_dve, 1)

            def w_lo(k, n):
                dve.wait_ge(whi_done, n)
                dve.tensor_tensor(sh_lo[:, k, :], sh_raw[:, k, :], sh_hi[:, k, :].bitcast(F32),
                                  ALU.subtract).then_inc(wlo_done, 1)

            softmax()
            best_expert()
            wbot_out(1)
            wbot_out(3)
            w_lo(0, 1)
            w_lo(1, 2)
            dve.wait_ge(l2_in, 16 * 5)

            def x1_out(g):
                c = slice(g * GT, (g + 1) * GT)
                dve.wait_ge(l0_done, g + 1)
                dve.scalar_tensor_tensor(out=xT[:, c], in0=yy[:, g, :], scalar=biases[:, 0:1], in1=xT[:, c],
                                         op0=ALU.add, op1=ALU.add).then_inc(x1_done, 1)

            x1_out(0)
            dve.wait_ge(x1hi_done, 1)
            dve.tensor_tensor(x_lo[:, 0:GT], xT[:, 0:GT], x_hi[:, 0:GT].bitcast(F32), ALU.subtract).then_inc(x1lo_dve, 1)
            x1_out(1)
            x1_out(2)
            w_lo(2, 3)

            def shared_prod(q, par, first):
                dve.wait_ge(sh_gelu_done, q + 1)
                dve.wait_ge(sh_u_done, q + 1)
                if not first:
                    dve.wait_ge(sh_lo_done, q - 1)
                dve.tensor_tensor(prod_s[:, par, :], gelu_s[:, par, :], gu[:, 2 + par, :],
                                  ALU.mult).then_inc(sh_prod_done, 1)

            def shared_lo(q, par, first):
                dve.wait_ge(sh_hi_done, q + 1)
                if not first:
                    dve.wait_ge(sh_dn_done, q - 1)
                dve.tensor_tensor(prod_lo[:, par, :], prod_s[:, par, :], prod_hi[:, par, :].bitcast(F32),
                                  ALU.subtract).then_inc(sh_lo_done, 1)

            def shared_y(g):
                c = bass.ds(g * GT, GT)
                dve.wait_ge(sh_dn_done, (g + 1) * NC)
                dve.tensor_tensor(yT[:, c], yy[:, bass.ds(g, 1), :].rearrange("p a n -> p (a n)"), xT[:, c],
                                  ALU.add).then_inc(sh_y_done, 1)

            def shared_group(g, first, routing=False):
                for c in range(NC):
                    shared_prod(g * NC + c, c % 2, first and c < 2)
                    if not (first and c == 0):
                        shared_lo(g * NC + c - 1, (c - 1) % 2, first and c < 3)
                    if first and c == 0:
                        second_value()
                    if first and c == 1:
                        x1_out(3)
                    if routing and c == 0:
                        second_expert()
                    if routing and c == 1:
                        pair_indices()
                    if routing and c == 3:
                        pair_weights()
                    if not first and c == 2:
                        shared_y(g - 1)

            shared_group(0, True)
            dve.wait_ge(whi_done, 4)
            dve.tensor_tensor(l2_lo[:], l2_raw[:, 0:2, :], l2_hi[:].bitcast(F32), ALU.subtract).then_inc(wlo_done, 1)
            shared_group(1, False, routing=True)
            with dve.Fori(2, NG) as g:
                shared_group(g, False)

            def pair_expert(p):
                return dve.value_load(pair_e_cols[0:1, bass.ds(p, 1)], min_val=0, max_val=E - 1)

            def copy_gu(p, k, e, first):
                if not first:
                    dve.wait_ge(ex_u_done, p - len(pair_gu) + 1)
                dve.tensor_copy(pair_gu[k], sk_gu[:, bass.ds(e, 1), :].rearrange("p a n -> p (a n)")
                                ).then_inc(gu_copied, 1)

            def expert_prod(p, k, first):
                dve.wait_ge(ex_gelu_done, p + 1)
                dve.wait_ge(ex_u_done, p + 1)
                if first:
                    dve.wait_ge(sh_lo_done, NG * NC)
                else:
                    dve.wait_ge(ex_dn_done, p - 1)
                dve.scalar_tensor_tensor(out=prod_s[:, k, :], in0=gelu_s[:, k, :], scalar=pair_w_cols[:, bass.ds(p, 1)],
                                         in1=gu[:, 2 + k, :], op0=ALU.mult, op1=ALU.mult).then_inc(ex_prod_done, 1)

            def x2_out(b, ypar):
                c = bass.ds(b * S, S)
                dve.wait_ge(ex_dn_done, (b + 1) * TOPK)
                dve.tensor_tensor(yT[:, c], yy[:, ypar, 0:S], yT[:, c], ALU.add).then_inc(x2_done, 1)

            def l2_lo_part(g):
                c = bass.ds(g * GT, GT)
                dve.wait_ge(l2_hi_done, g + 1)
                dve.tensor_tensor(x_lo[:, c], yT[:, c], x_hi[:, c].bitcast(F32), ALU.subtract).then_inc(l2_lo_done, 1)

            def l2_scale(g):
                dve.wait_ge(l2_h_done, g + 1)
                dve.tensor_tensor(lora_h[:], yy[:, 2, :].rearrange("p (b s) -> p b s", s=S),
                                  cond_rep2[:, bass.ds(g * BG, BG)].rearrange("p (b o) -> p b o", o=1)
                                  .broadcast_to([P, BG, S]), ALU.mult).then_inc(l2_hs_done, 1)

            def x3_out(g):
                c = bass.ds(g * GT, GT)
                dve.wait_ge(l2_x_done, g + 1)
                dve.scalar_tensor_tensor(out=x3T[:, c], in0=yy[:, 3, :], scalar=biases[:, 1:2], in1=yT[:, c],
                                         op0=ALU.add, op1=ALU.add).then_inc(x3_done, 1)

            def expert_group(g, first=False, last=False):
                for j in range(PG):
                    p = g * PG + j
                    if not (first and j == 0):
                        expert_prod(p - 1, (j - 1) % TOPK, first and j < 3)
                    if not (last and j == PG - 1) and not (first and j == 0):
                        copy_gu(p + 1, (j + 1) % len(pair_gu), pair_expert(p + 1), first and j + 1 < len(pair_gu))
                    if j % 2 == 1 and not (first and j == 1):
                        x2_out(g * BG + (j - 3) // 2, ((j - 3) // 2) % 2)
                    if not first:
                        if j == 2:
                            l2_lo_part(g - 1)
                        elif j == 5:
                            l2_scale(g - 1)
                        elif j == 7:
                            x3_out(g - 1)

            dve.wait_ge(route_ready, 1)
            dve.wait_ge(skill_in, 16 * N_SKILL)
            shared_lo(NG * NC - 1, 1, False)
            copy_gu(1, 1, pair_expert(1), True)
            shared_y(NG - 1)
            dve.wait_ge(sh_y_done, NG)
            dve.wait_ge(setup_dve, 2)
            expert_group(0, first=True)
            with dve.Fori(1, NG - 1) as g:
                expert_group(g)
            expert_group(NG - 1, last=True)

            def batch_expert(b):
                return dve.value_load(best_e[0:1, bass.ds(b, 1)], min_val=0, max_val=E - 1)

            def copy_w3(b, j, e, first):
                if not first:
                    dve.wait_ge(gate3_done, b - BG + 1)
                dve.tensor_copy(batch_w3[:, j, 0:2 * H3], w3[:, bass.ds(e, 1), 0:2 * H3]
                                .rearrange("p a n -> p (a n)")).then_inc(w3_copied, 1)

            def hidden3(b, j, first):
                dve.wait_ge(gate3_done, b + 1)
                if not first:
                    dve.wait_ge(dn3_done, b - BG + 1)
                for c in range(NC3):
                    cs = slice(c * S, (c + 1) * S)
                    dve.wait_ge(silu_done, b * NC3 + c + 1)
                    dve.scalar_tensor_tensor(out=hid3[:, j, cs], in0=gu[:, 2 + j % 2, cs],
                                             scalar=bias3[:, bass.ds(b * NB3 + NC3 + c, 1)], in1=silu_s[:, j % 2, cs],
                                             op0=ALU.add, op1=ALU.mult).then_inc(hid3_done, 1)

            def out3(b, j):
                c = bass.ds(b * S, S)
                dve.wait_ge(dn3_done, b + 1)
                dve.scalar_tensor_tensor(out=x3T[:, c], in0=yy[:, j % 2, 0:S], scalar=bias3[:, bass.ds(b * NB3 + 2 * NC3, 1)],
                                         in1=x3T[:, c], op0=ALU.add, op1=ALU.add).then_inc(out_done, 1)

            def l3_group(g, first=False, last=False):
                for j in range(BG):
                    b = g * BG + j
                    if first and j == 0:
                        x2_out(B - 1, (B - 1) % 2)
                        l2_lo_part(NG - 1)
                    else:
                        hidden3(b - 1, (j - 1) % BG, first)
                    if j == first:
                        e = batch_expert(b + 1)
                    if not (last and j == BG - 1) and not (first and j == 0):
                        copy_w3(b + 1, (j + 1) % BG, e, first and j < BG - 1)
                        if j < BG - 2 + (not last):
                            e = batch_expert(b + 2)
                    if not (first and j < 3):
                        out3(b - 3, (j - 3) % BG)
                    if first and j == 2:
                        l2_scale(NG - 1)

            dve.wait_ge(w3_in, 16 * N_W3)
            copy_w3(0, 0, batch_expert(0), True)
            expert_prod(NP - 1, TOPK - 1, False)
            copy_w3(1, 1, batch_expert(1), True)
            dve.wait_ge(b3_copied, B)
            l3_group(0, first=True)
            x3_out(NG - 1)
            with dve.Fori(1, NG - 1) as g:
                l3_group(g)
            l3_group(NG - 1, last=True)
            hidden3(B - 1, BG - 1, False)
            out3(B - 3, BG - 3)
            out3(B - 2, BG - 2)
            out3(B - 1, BG - 1)


def kernel(x, cond_8, L0_cond_weight, L0_cond_mask, L0_cond_bias, L1_cond_skill_gate, L1_cond_skill_up,
           L1_cond_skill_down, L1_cond_shared_gate, L1_cond_shared_up, L1_cond_shared_down, L2_cond_W_base,
           L2_cond_b_base, L2_cond_As, L2_cond_Bs, L3_cond_W_up, L3_cond_b_up, L3_cond_W_gate, L3_cond_b_gate,
           L3_cond_W_down, L3_cond_b_down):
    import numpy as np
    import concourse.bacc as bacc
    from concourse.bass_utils import run_bass_kernel_spmd

    B, S, D = x.shape
    E = cond_8.shape[1]
    OI = D // E
    H3 = L3_cond_W_up.shape[1]

    def lay(a, *axes):
        a = np.asarray(a)
        return np.ascontiguousarray(a.transpose(*axes) if axes else a)

    def by_partition(b):
        b = np.asarray(b)
        return np.ascontiguousarray(b.reshape(E, -1, D).transpose(2, 0, 1))

    ins = {
        "xT": lay(x, 2, 0, 1).reshape(D, B * S),
        "cond": lay(cond_8),
        "condT": lay(cond_8, 1, 0),
        "w0": lay(np.asarray(L0_cond_weight).reshape(E, D // OI, OI, D), 0, 2, 1, 3).reshape(D, -1),
        "mask": lay(np.asarray(L0_cond_mask).reshape(D // OI, OI, D), 1, 0, 2).reshape(OI, -1),
        "bias0": lay(L0_cond_bias).reshape(D, 1),
        "sk_gate": lay(L1_cond_skill_gate),
        "sk_up": lay(L1_cond_skill_up),
        "sk_down": lay(L1_cond_skill_down),
        "sh_gate": lay(L1_cond_shared_gate),
        "sh_up": lay(L1_cond_shared_up),
        "sh_down": lay(L1_cond_shared_down),
        "wbase": lay(L2_cond_W_base, 1, 0),
        "bbase": lay(L2_cond_b_base).reshape(D, 1),
        "lora_a": lay(L2_cond_As, 2, 0, 1).reshape(D, -1),
        "lora_b": lay(L2_cond_Bs, 0, 2, 1).reshape(D, -1),
        "w3": np.concatenate([
            lay(L3_cond_W_up, 2, 0, 1), lay(L3_cond_W_gate, 2, 0, 1),
            lay(np.asarray(L3_cond_W_down).reshape(E, D, H3 // D, D), 3, 0, 2, 1).reshape(D, E, H3)], axis=2),
        "b3": np.concatenate([by_partition(b) for b in (L3_cond_b_up, L3_cond_b_gate, L3_cond_b_down)], axis=2),
    }
    nc = bacc.Bacc("TRN2", target_bir_lowering=False, num_devices=1)
    aps = [nc.dram_tensor(n + "_dram", a.shape, mybir.dt.from_np(a.dtype), kind="ExternalInput").ap() for n, a in ins.items()]
    out = nc.dram_tensor("outT_dram", (D, B * S), F32, kind="ExternalOutput").ap()
    cond_resid_kernel(nc, *aps, out)
    r = run_bass_kernel_spmd(nc, [{n + "_dram": a for n, a in ins.items()}], core_ids=[0])
    got = r.results[0]["outT_dram"]
    return np.ascontiguousarray(got.reshape(D, B, S).transpose(1, 2, 0))
```

```python
from contextlib import ExitStack

import concourse.bass as bass
from concourse import mybir

F32 = mybir.dt.float32
F32R = mybir.dt.float32r
I32 = mybir.dt.int32
ALU = mybir.AluOpType
ACT = mybir.ActivationFunctionType
AX = mybir.AxisListType

P = 128


def cond_resid_kernel(
    nc, xT_d, cond_d, condT_d, w0_d, mask_d, bias0_d,
    sk_gate_d, sk_up_d, sk_down_d, sh_gate_d, sh_up_d, sh_down_d,
    wbase_d, bbase_d, lora_a_d, lora_b_d,
    w3_d, b3_d, outT_d,
):
    TOK = xT_d.shape[1]
    B, E = cond_d.shape
    S = TOK // B
    I = sh_gate_d.shape[1]
    NC = I // P
    H3 = w3_d.shape[2] // 3
    NC3 = H3 // P
    GT = 512
    NG = TOK // GT
    BG = GT // S
    TOPK = 2
    PG = BG * TOPK
    NP = B * TOPK
    OI = P // E
    OB = P // OI
    W3_SLOTS = 8
    WARM = 20
    LORA_SCALE = 2.0
    MOE_SCALE = 1.0 / 12
    W3 = 3 * H3
    NB3 = 2 * NC3 + 1
    assert S == P and B * E == P and NG == 4 and NC == 4 and NC3 == 2 and BG == 4

    with ExitStack() as ctx:
        def sb(name, shape, dt=F32):
            return ctx.enter_context(nc.sbuf_tensor(name, shape, dt))

        def sem(name):
            return ctx.enter_context(nc.semaphore(name))

        xT = sb("xT", [P, TOK])
        x_hi = sb("x_hi", [P, TOK], F32R)
        x_lo = sb("x_lo", [P, TOK], F32R)
        yT = sb("yT", [P, TOK])
        x3T = sb("x3T", [P, TOK])
        w0 = sb("w0", [P, OB * P])
        mask = sb("mask", [P, OB * P])
        cond_rep = sb("cond_rep", [P, B])
        cond_rep2 = sb("cond_rep2", [P, B])
        delta16 = sb("delta16", [P, OI])
        y_kron = sb("y_kron", [P, B, OI])
        wbotT = sb("wbotT", [P, B, P])
        ident = sb("ident", [P, P])
        spare = sb("spare", [P, 1])
        biases = sb("biases", [P, 2])
        cond_bc = sb("cond_bc", [P, B, E])
        rev = sb("rev", [P, E])
        rev_i = sb("rev_i", [P, E], I32)
        r_a = sb("r_a", [P, B, E])
        r_b = sb("r_b", [P, B, E])
        r_w = sb("r_w", [P, B, E])
        r_w2 = sb("r_w2", [P, B, E])
        r_s = sb("r_s", [P, 8, B])
        pair_w0 = sb("pair_w0", [P, B, TOPK])
        pair_w1 = sb("pair_w1", [P, B, TOPK])
        pair_w = sb("pair_w", [P, B, TOPK])
        pair_e = sb("pair_e", [P, B, TOPK], I32)
        best_e = sb("best_e", [P, B], I32)
        sh_raw = sb("sh_raw", [P, 3, I])
        sh_hi = sb("sh_hi", [P, 3, I], F32R)
        sh_lo = sb("sh_lo", [P, 3, I], F32R)
        gelu_s = sb("gelu_s", [P, 2, GT])
        prod_s = sb("prod_s", [P, 2, GT])
        prod_hi = sb("prod_hi", [P, 2, GT], F32R)
        prod_lo = sb("prod_lo", [P, 2, GT], F32R)
        sk_gu = sb("sk_gu", [P, E, 2 * I])
        sk_dn = sb("sk_dn", [P, E, I])
        pair_gu_buf = sb("pair_gu", [P, 2, 2 * I])
        pair_dn = sb("pair_dn", [P, 2, I])
        wbot_place = wbotT[:].rearrange("p b o -> p (b o)")
        pair_gu = [pair_gu_buf[:, 0, :], pair_gu_buf[:, 1, :], wbot_place[:, 0:2 * I], wbot_place[:, 2 * I:4 * I]]
        l2_raw = sb("l2_raw", [P, 3, P])
        l2_hi = sb("l2_hi", [P, 2, P], F32R)
        l2_lo = sb("l2_lo", [P, 2, P], F32R)
        lora_h = sb("lora_h", [P, BG, S])
        w3 = sb("w3", [P, W3_SLOTS, W3])
        b3 = sb("b3", [P, E, NB3])
        batch_b3 = sb("batch_b3", [P, B, NB3])
        silu_s = sb("silu_s", [P, 2, H3])
        hid3 = sb("hid3", [P, BG, H3])

        gu = ctx.enter_context(nc.psum_tensor("gu", [P, 4, GT], F32))
        yy = ctx.enter_context(nc.psum_tensor("yy", [P, 4, GT], F32))

        cond_in, w0_in, mask_in, x_in = sem("cond_in"), sem("w0_in"), sem("mask_in"), sem("x_in")
        shgu_in, shdn_in, l2_in, skill_in, b3_in = (
            sem("shgu_in"), sem("shdn_in"), sem("l2_in"), sem("skill_in"), sem("b3_in"))
        out_stored = sem("out_stored")
        pool_const = sem("pool_const")
        route_step = sem("route_step")
        exp_ready, exp_in_ready, route_ready = sem("exp_ready"), sem("exp_in_ready"), sem("route_ready")
        setup_dve = sem("setup_dve")
        kron_ready, masked_ready = sem("kron_ready"), sem("masked_ready")
        wbot_done, wbot_act, wbot_dve = sem("wbot_done"), sem("wbot_act"), sem("wbot_dve")
        l0_done, x1_done, x1hi_done, x1lo_dve, x1lo_pool = (
            sem("l0_done"), sem("x1_done"), sem("x1hi_done"), sem("x1lo_dve"), sem("x1lo_pool"))
        whi_done, wlo_done = sem("whi_done"), sem("wlo_done")
        sh_g_done, sh_u_done, sh_dn_done = sem("sh_g_done"), sem("sh_u_done"), sem("sh_dn_done")
        sh_gelu_done, sh_prod_done, sh_hi_done, sh_lo_done, sh_y_done = (
            sem("sh_gelu_done"), sem("sh_prod_done"), sem("sh_hi_done"), sem("sh_lo_done"), sem("sh_y_done"))
        gu0_copied = sem("gu0_copied")
        gu_copied, dn_copied = sem("gu_copied"), sem("dn_copied")
        ex_g_done, ex_u_done, ex_dn_done = sem("ex_g_done"), sem("ex_u_done"), sem("ex_dn_done")
        ex_gelu_done, ex_prod_done, x2_done = sem("ex_gelu_done"), sem("ex_prod_done"), sem("x2_done")
        l2_hi_done, l2_lo_done, l2_h_done, l2_hs_done, l2_x_done, x3_done = (
            sem("l2_hi_done"), sem("l2_lo_done"), sem("l2_h_done"), sem("l2_hs_done"), sem("l2_x_done"), sem("x3_done"))
        w3_slot_in = [sem(f"w3_slot_in{i}") for i in range(W3_SLOTS)]
        b3_copied, best_ready = sem("b3_copied"), sem("best_ready")
        up3_done, gate3_done, dn3_done = sem("up3_done"), sem("gate3_done"), sem("dn3_done")
        silu_done, hid3_done, out_done = sem("silu_done"), sem("hid3_done"), sem("out_done")

        assert wbot_place.shape[1] == 4 * I
        N_SKILL = 3 * E
        N_B3 = 1

        def cols(i, n):
            return bass.ds(i * n, n)

        bias3 = batch_b3[:].rearrange("p b n -> p (b n)")
        pair_w_cols = pair_w[:].rearrange("p b k -> p (b k)")
        pair_e_cols = pair_e[:].rearrange("p b k -> p (b k)")
        block = ctx.enter_context(nc.Block())

        @block.sync
        def _(sp):
            sp.dma_start(cond_rep[:], bass.AP(condT_d.tensor, 0, [[B, E], [0, OI], [1, B]])).then_inc(cond_in, 16)
            sp.dma_start(w0[:], w0_d).then_inc(w0_in, 16)
            for g in range(NG):
                sp.dma_start(xT[:, g * GT:(g + 1) * GT], xT_d[:, g * GT:(g + 1) * GT]).then_inc(x_in, 16)
            sp.dma_start(sh_raw[:, 0, :], sh_gate_d).then_inc(shgu_in, 16)
            sp.dma_start(sh_raw[:, 1, :], sh_up_d).then_inc(shgu_in, 16)
            sp.dma_start(sh_raw[:, 2, :].rearrange("p (c h) -> p c h", c=NC),
                         sh_down_d.rearrange("(c p) h -> p c h", p=P)).then_inc(shdn_in, 16)
            sp.dma_start(l2_raw[:, 0, :], wbase_d).then_inc(l2_in, 16)
            sp.dma_start(l2_raw[:, 1, :], lora_a_d).then_inc(l2_in, 16)
            sp.dma_start(l2_raw[:, 2, :], lora_b_d).then_inc(l2_in, 16)
            for e in range(E):
                sp.dma_start(sk_gu[:, e, 0:I], sk_gate_d[e]).then_inc(skill_in, 16)
                sp.dma_start(sk_gu[:, e, I:2 * I], sk_up_d[e]).then_inc(skill_in, 16)
                sp.dma_start(sk_dn[:, e, :].rearrange("p (c h) -> p c h", c=NC),
                             sk_down_d[e].rearrange("(c p) h -> p c h", p=P)).then_inc(skill_in, 16)
            sp.dma_start(b3[:], b3_d).then_inc(b3_in, 16)

            def load_w3(b):
                e = sp.value_load(best_e[0:1, b:b + 1], min_val=0, max_val=E - 1)
                sp.dma_start(w3[:, b % W3_SLOTS, :], w3_d[bass.ds(e, 1)].rearrange("a p n -> p (a n)")
                             ).then_inc(w3_slot_in[b % W3_SLOTS], 16)

            def store(b0, b1):
                sp.wait_ge(out_done, b1)
                sp.dma_start(outT_d[:, b0 * S:b1 * S], x3T[:, b0 * S:b1 * S]).then_inc(out_stored, 16)

            sp.wait_ge(best_ready, 1)
            for b in range(W3_SLOTS):
                load_w3(b)
            for b in range(W3_SLOTS, B):
                sp.wait_ge(dn3_done, b - W3_SLOTS + 1)
                load_w3(b)
                if b % BG == BG - 1:
                    store(b - W3_SLOTS - BG + 1, b - W3_SLOTS + 1)
            for b0, b1 in ((8, 12), (12, 15), (15, 16)):
                store(b0, b1)
            sp.wait_ge(out_stored, 16 * 5)

        @block.gpsimd
        def _(pool):
            pool.memset(ident[:], 0.0).then_inc(pool_const, 1)
            pool.iota(rev_i[:], [[-1, E]], base=E, channel_multiplier=0).then_inc(pool_const, 1)
            pool.wait_ge(pool_const, 2)
            pool.affine_select(out=ident[:], in_=ident[:], compare_op=ALU.not_equal, fill=1.0, base=0,
                               pattern=[[-1, P]], channel_multiplier=1).then_inc(pool_const, 1)
            for g in range(1, NG):
                c = slice(g * GT, (g + 1) * GT)
                pool.wait_ge(x1hi_done, g + 1)
                pool.tensor_tensor(x_lo[:, c], xT[:, c], x_hi[:, c].bitcast(F32), ALU.subtract).then_inc(x1lo_pool, 1)
            pool.wait_ge(route_ready, 1)
            pool.wait_ge(skill_in, 16 * N_SKILL)
            e = pool.value_load(pair_e_cols[0:1, 0:1], min_val=0, max_val=E - 1)
            pool.tensor_copy(pair_gu[0], sk_gu[:, bass.ds(e, 1), :].rearrange("p a n -> p (a n)")
                             ).then_inc(gu0_copied, 1)
            pool.wait_ge(best_ready, 1)
            pool.wait_ge(b3_in, 16 * N_B3)
            with pool.Fori(0, B) as b:
                e = pool.value_load(best_e[0:1, bass.ds(b, 1)], min_val=0, max_val=E - 1)
                pool.tensor_copy(batch_b3[:, bass.ds(b, 1), :].rearrange("p a n -> p (a n)"),
                                 b3[:, bass.ds(e, 1), :].rearrange("p a n -> p (a n)")).then_inc(b3_copied, 1)

        @block.tensor
        def _(pe):
            def split3(out, w_hi, w_lo, m_hi, m_lo, start, stop):
                pe.matmul(out, w_hi, m_hi, start=start, stop=False)
                pe.matmul(out, w_hi, m_lo, start=False, stop=False)
                return pe.matmul(out, w_lo, m_hi, start=False, stop=stop)

            pe.wait_ge(pool_const, 3)
            for _ in range(WARM):
                pe.matmul(yy[:, 0, 0:P], ident[:], ident[:], start=True, stop=True)
            pe.wait_ge(kron_ready, 1)
            pe.wait_ge(masked_ready, 1)
            for ob in range(OB):
                place = yy[:, 3, 0:B * OI] if ob == OB - 1 else gu[:, ob // 2, (ob % 2) * B * OI:(ob % 2 + 1) * B * OI]
                pe.matmul(place, w0[:, ob * P:(ob + 1) * P],
                          y_kron[:].rearrange("p b o -> p (b o)"), start=True, stop=True).then_inc(wbot_done, 1)
            pe.wait_ge(wbot_act, 3)
            pe.wait_ge(wbot_dve, 2)
            for g in range(NG):
                pe.wait_ge(x_in, 16 * NG)
                for b in range(g * BG, (g + 1) * BG):
                    mm = pe.matmul(yy[:, g, (b % BG) * S:(b % BG + 1) * S], wbotT[:, b, :], xT[:, b * S:(b + 1) * S],
                                   start=True, stop=True)
                mm.then_inc(l0_done, 1)

            def shared_up(g, c, first):
                q = g * NC + c
                tok = bass.ds(g * GT, GT)
                ch = slice(c * P, (c + 1) * P)
                if not (first and c < 2):
                    pe.wait_ge(sh_gelu_done, q - 1)
                split3(gu[:, c % 2, :], sh_hi[:, 0, ch], sh_lo[:, 0, ch], x_hi[:, tok], x_lo[:, tok],
                       True, True).then_inc(sh_g_done, 1)
                if not (first and c < 2):
                    pe.wait_ge(sh_prod_done, q - 1)
                split3(gu[:, 2 + c % 2, :], sh_hi[:, 1, ch], sh_lo[:, 1, ch], x_hi[:, tok], x_lo[:, tok],
                       True, True).then_inc(sh_u_done, 1)

            def shared_down(g, c):
                q = g * NC + c
                ch = slice(c * P, (c + 1) * P)
                pe.wait_ge(sh_hi_done, q + 1)
                pe.wait_ge(sh_lo_done, q + 1)
                out = yy[:, bass.ds(g, 1), :].rearrange("p a n -> p (a n)")
                split3(out, sh_hi[:, 2, ch], sh_lo[:, 2, ch], prod_hi[:, c % 2, :], prod_lo[:, c % 2, :],
                       c == 0, c == NC - 1).then_inc(sh_dn_done, 1)

            def shared_group(g, first):
                pe.wait_ge(x1hi_done, g + 1)
                if first:
                    pe.wait_ge(x1lo_dve, 1)
                else:
                    pe.wait_ge(x1lo_pool, g)
                for c in range(NC):
                    shared_up(g, c, first)
                    if c >= 2:
                        shared_down(g, c - 2)
                    elif not first:
                        shared_down(g - 1, c + NC - 2)

            pe.wait_ge(whi_done, 2)
            pe.wait_ge(wlo_done, 2)
            shared_group(0, True)
            with pe.Fori(1, NG) as g:
                shared_group(g, False)

            def expert_up(b, k, par, first):
                p = b * TOPK + k
                w = pair_gu[par % len(pair_gu)]
                if first and par == 0:
                    pe.wait_ge(gu0_copied, 1)
                else:
                    pe.wait_ge(gu_copied, p)
                tok = bass.ds(b * S, S)
                if first and par < 2:
                    pe.wait_ge(sh_gelu_done, NG * NC - 1 + par)
                else:
                    pe.wait_ge(ex_gelu_done, p - 1)
                for c in range(NC):
                    mm = pe.matmul(gu[:, k, c * S:(c + 1) * S], w[:, c * P:(c + 1) * P], xT[:, tok],
                                   start=True, stop=True)
                mm.then_inc(ex_g_done, 1)
                if first and par < 2:
                    pe.wait_ge(sh_prod_done, NG * NC - 1 + par)
                else:
                    pe.wait_ge(ex_prod_done, p - 1)
                for c in range(NC):
                    mm = pe.matmul(gu[:, 2 + k, c * S:(c + 1) * S], w[:, I + c * P:I + (c + 1) * P],
                                   xT[:, tok], start=True, stop=True)
                mm.then_inc(ex_u_done, 1)

            def expert_down(b, k, ypar, first):
                p = b * TOPK + k
                pe.wait_ge(ex_prod_done, p + 1)
                pe.wait_ge(dn_copied, p + 1)
                if k == 0:
                    if first:
                        pe.wait_ge(sh_y_done, ypar + 1)
                    else:
                        pe.wait_ge(x2_done, b - 1)
                for c in range(NC):
                    mm = pe.matmul(yy[:, ypar, 0:S], pair_dn[:, k, c * P:(c + 1) * P],
                                   prod_s[:, k, c * S:(c + 1) * S],
                                   start=(k == 0 and c == 0), stop=(k == TOPK - 1 and c == NC - 1))
                mm.then_inc(ex_dn_done, 1)

            def lora_in(g):
                tok = bass.ds(g * GT, GT)
                pe.wait_ge(l2_hi_done, g + 1)
                pe.wait_ge(l2_lo_done, g + 1)
                split3(yy[:, 2, :], l2_hi[:, 1, :], l2_lo[:, 1, :], x_hi[:, tok], x_lo[:, tok],
                       True, True).then_inc(l2_h_done, 1)
                split3(yy[:, 3, :], l2_hi[:, 0, :], l2_lo[:, 0, :], x_hi[:, tok], x_lo[:, tok], True, False)

            def lora_out(g):
                pe.wait_ge(l2_hs_done, g + 1)
                pe.matmul(yy[:, 3, :], l2_raw[:, 2, :], lora_h[:].rearrange("p b s -> p (b s)"),
                          start=False, stop=True).then_inc(l2_x_done, 1)

            def expert_group(g, first):
                for j in range(PG):
                    b, k = g * BG + j // TOPK, j % TOPK
                    if not (first and j == 0):
                        expert_up(b, k, j, first)
                    if j >= 1:
                        jb, jk = (j - 1) // TOPK, (j - 1) % TOPK
                        expert_down(g * BG + jb, jk, jb % 2, first and jb < 2)
                    elif not first:
                        expert_down(g * BG - 1, TOPK - 1, (BG - 1) % 2, False)
                    if not first and j == 4:
                        lora_in(g - 1)
                    if not first and j == 6:
                        lora_out(g - 1)

            expert_up(0, 0, 0, True)
            shared_down(NG - 1, NC - 2)
            shared_down(NG - 1, NC - 1)
            expert_group(0, True)
            pe.wait_ge(whi_done, 4)
            pe.wait_ge(wlo_done, 4)
            pe.wait_ge(sh_y_done, NG)
            with pe.Fori(1, NG) as g:
                expert_group(g, False)

            def up3(b):
                w = w3[:, b % W3_SLOTS, :]
                tok = slice(b * S, (b + 1) * S)
                pe.wait_ge(w3_slot_in[b % W3_SLOTS], 16 * (b // W3_SLOTS + 1))
                pe.wait_ge(x3_done, b // BG + 1)
                if b < 2:
                    pe.wait_ge(ex_gelu_done, NP - 1 + b)
                else:
                    pe.wait_ge(silu_done, (b - 1) * NC3)
                for c in range(NC3):
                    mm = pe.matmul(gu[:, b % 2, c * S:(c + 1) * S], w[:, c * P:(c + 1) * P], x3T[:, tok],
                                   start=True, stop=True)
                mm.then_inc(up3_done, 1)
                if b < 2:
                    pe.wait_ge(ex_prod_done, NP - 1 + b)
                else:
                    pe.wait_ge(hid3_done, (b - 1) * NC3)
                for c in range(NC3):
                    mm = pe.matmul(gu[:, 2 + b % 2, c * S:(c + 1) * S], w[:, H3 + c * P:H3 + (c + 1) * P],
                                   x3T[:, tok], start=True, stop=True)
                mm.then_inc(gate3_done, 1)

            def down3(b):
                w = w3[:, b % W3_SLOTS, 2 * H3:]
                if b < 2:
                    pe.wait_ge(x2_done, B - 1 + b)
                else:
                    pe.wait_ge(out_done, b - 1)
                for c in range(NC3):
                    pe.wait_ge(hid3_done, b * NC3 + c + 1)
                    mm = pe.matmul(yy[:, b % 2, 0:S], w[:, c * P:(c + 1) * P], hid3[:, b % BG, c * S:(c + 1) * S],
                                   start=(c == 0), stop=(c == NC3 - 1))
                mm.then_inc(dn3_done, 1)

            for b in range(B):
                up3(b)
                if b == 0:
                    expert_down(B - 1, TOPK - 1, (B - 1) % 2, False)
                if b >= 2:
                    down3(b - 2)
                if b == 2:
                    lora_in(NG - 1)
                if b == 3:
                    lora_out(NG - 1)
            down3(B - 2)
            down3(B - 1)

        @block.scalar
        def _(act):
            act.dma_start(cond_bc[:].rearrange("p b e -> p (b e)"),
                          bass.AP(cond_d.tensor, 0, [[0, P], [1, B * E]])).then_inc(cond_in, 16)
            act.dma_start(mask[:], bass.AP(mask_d.tensor, 0, [[0, E], [OB * P, OI], [1, OB * P]])).then_inc(mask_in, 16)
            act.dma_start(biases[:, 0:1], bias0_d).then_inc(l2_in, 16)
            act.dma_start(biases[:, 1:2], bbase_d).then_inc(l2_in, 16)
            act.wait_ge(exp_in_ready, 1)
            act.activation(r_b[:], r_a[:], ACT.Exp).then_inc(exp_ready, 1)
            act.wait_ge(pool_const, 3)
            act.activation(spare[:], ident[:, 0:1], ACT.Gelu_apprx_tanh)
            def wbot_out(k):
                act.wait_ge(wbot_done, 2 * k + 2)
                act.activation(wbotT[:, :, 2 * k * OI:(2 * k + 2) * OI].rearrange("p b (a o) -> p a b o", a=2),
                               gu[:, k, :].rearrange("p (a b o) -> p a b o", a=2, b=B), ACT.Copy).then_inc(wbot_act, 1)

            wbot_out(0)
            act.wait_ge(shgu_in, 32)
            act.activation(sh_hi[:, 0, :], sh_raw[:, 0, :], ACT.Copy).then_inc(whi_done, 1)
            wbot_out(2)
            act.wait_ge(wbot_done, OB)
            act.activation(wbotT[:, :, (OB - 1) * OI:OB * OI],
                           yy[:, 3, 0:B * OI].rearrange("p (b o) -> p b o", b=B), ACT.Copy).then_inc(wbot_act, 1)
            act.activation(sh_hi[:, 1, :], sh_raw[:, 1, :], ACT.Copy).then_inc(whi_done, 1)

            def x1_hi(g):
                c = slice(g * GT, (g + 1) * GT)
                act.wait_ge(x1_done, g + 1)
                act.activation(x_hi[:, c], xT[:, c], ACT.Copy).then_inc(x1hi_done, 1)

            x1_hi(0)
            act.wait_ge(shdn_in, 16)
            act.activation(sh_hi[:, 2, :], sh_raw[:, 2, :], ACT.Copy).then_inc(whi_done, 1)
            x1_hi(1)

            def shared_gelu(q, par, first):
                act.wait_ge(sh_g_done, q + 1)
                if not first:
                    act.wait_ge(sh_prod_done, q - 1)
                act.activation(gelu_s[:, par, :], gu[:, par, :], ACT.Gelu_apprx_tanh).then_inc(sh_gelu_done, 1)

            def shared_hi(q, par, first):
                act.wait_ge(sh_prod_done, q + 1)
                if not first:
                    act.wait_ge(sh_dn_done, q - 1)
                act.activation(prod_hi[:, par, :], prod_s[:, par, :], ACT.Copy).then_inc(sh_hi_done, 1)

            def shared_group(g, first):
                for c in range(NC):
                    if first and c == 1:
                        shared_hi(0, 0, True)
                    shared_gelu(g * NC + c, c % 2, first and c < 2)
                    if not (first and c < 2):
                        shared_hi(g * NC + c - 1, (c - 1) % 2, first and c < 3)
                    if first and 1 <= c <= 2:
                        x1_hi(c + 1)

            shared_group(0, True)
            act.wait_ge(l2_in, 16 * 5)
            act.activation(l2_hi[:], l2_raw[:, 0:2, :], ACT.Copy).then_inc(whi_done, 1)
            with act.Fori(1, NG) as g:
                shared_group(g, False)

            def pair_expert(p):
                return act.value_load(pair_e_cols[0:1, bass.ds(p, 1)], min_val=0, max_val=E - 1)

            def copy_down(p, k, e, first):
                if not first:
                    act.wait_ge(ex_dn_done, p - 1)
                act.activation(pair_dn[:, k, :], sk_dn[:, bass.ds(e, 1), :].rearrange("p a n -> p (a n)"),
                               ACT.Copy).then_inc(dn_copied, 1)

            def expert_gelu(p, k, first):
                act.wait_ge(ex_g_done, p + 1)
                if not first:
                    act.wait_ge(ex_prod_done, p - 1)
                act.activation(gelu_s[:, k, :], gu[:, k, :], ACT.Gelu_apprx_tanh).then_inc(ex_gelu_done, 1)

            def l2_split(g):
                c = bass.ds(g * GT, GT)
                act.wait_ge(x2_done, (g + 1) * BG)
                act.activation(x_hi[:, c], yT[:, c], ACT.Copy).then_inc(l2_hi_done, 1)

            def expert_group(g, first):
                for j in range(PG):
                    if not (first and j == 0):
                        expert_gelu(g * PG + j - 1, (j - 1) % TOPK, first and j < 3)
                        if j == first:
                            e = pair_expert(g * PG + j)
                        copy_down(g * PG + j, j % TOPK, e, first and j < 2)
                        if j < PG - 1:
                            e = pair_expert(g * PG + j + 1)
                    if not first and j == 2:
                        l2_split(g - 1)

            act.wait_ge(route_ready, 1)
            act.wait_ge(skill_in, 16 * N_SKILL)
            copy_down(0, 0, pair_expert(0), True)
            shared_hi(NG * NC - 1, 1, False)
            expert_group(0, True)
            with act.Fori(1, NG) as g:
                expert_group(g, False)

            def silu3(b, j, first):
                act.wait_ge(up3_done, b + 1)
                if not first:
                    act.wait_ge(hid3_done, (b - 1) * NC3)
                for c in range(NC3):
                    cs = slice(c * S, (c + 1) * S)
                    act.activation(silu_s[:, j % 2, cs], gu[:, j % 2, cs], ACT.Silu,
                                   bias=bias3[:, bass.ds(b * NB3 + c, 1)]).then_inc(silu_done, 1)

            def l3_group(g, first=False):
                for j in range(BG):
                    b = g * BG + j
                    if not (first and j == 0):
                        silu3(b - 1, (j - 1) % BG, first and j < 3)
                    if first and j == 1:
                        l2_split(NG - 1)

            expert_gelu(NP - 1, TOPK - 1, False)
            act.activation(spare[:], ident[:, 0:1], ACT.Silu)
            act.wait_ge(b3_copied, B)
            l3_group(0, first=True)
            with act.Fori(1, NG) as g:
                l3_group(g)
            silu3(B - 1, BG - 1, False)

        @block.vector
        def _(dve):
            step = [0]

            def link(ins):
                step[0] += 1
                ins.then_inc(route_step, 1)
                dve.wait_ge(route_step, step[0])

            def over_e(a):
                return a.rearrange("p (b o) -> p b o", o=1).broadcast_to([P, B, E])

            def over_b(a):
                return a.rearrange("p (o e) -> p o e", o=1).broadcast_to([P, B, E])

            cmax, esum, rsum, best, bestr, sec, secr, topr = (r_s[:, i, :] for i in range(8))

            def top_expert():
                link(dve.tensor_tensor(r_w2[:], cond_bc[:], over_e(cmax), ALU.is_equal))
                link(dve.tensor_tensor(r_w2[:], r_w2[:], over_b(rev[:]), ALU.mult))
                link(dve.tensor_reduce(topr, r_w2[:], AX.X, ALU.max))
                dve.tensor_scalar(best_e[:], topr, -1.0, float(E), ALU.mult, ALU.add).then_inc(best_ready, 1)

            def softmax():
                dve.wait_ge(exp_ready, 1)
                link(dve.tensor_reduce(esum, r_b[:], AX.X, ALU.add))
                link(dve.reciprocal(rsum, esum))
                link(dve.tensor_tensor(r_w[:], r_b[:], over_e(rsum), ALU.mult))

            def best_expert():
                link(dve.tensor_reduce(best, r_w[:], AX.X, ALU.max))
                link(dve.tensor_tensor(r_a[:], r_w[:], over_e(best), ALU.is_equal))
                link(dve.tensor_tensor(r_a[:], r_a[:], over_b(rev[:]), ALU.mult))
                link(dve.tensor_reduce(bestr, r_a[:], AX.X, ALU.max))

            def second_value():
                link(dve.tensor_tensor(r_a[:], over_b(rev[:]), over_e(bestr), ALU.is_equal))
                link(dve.scalar_tensor_tensor(out=r_w2[:], in0=r_a[:], scalar=-2.0, in1=r_w[:],
                                              op0=ALU.mult, op1=ALU.add))
                link(dve.tensor_reduce(sec, r_w2[:], AX.X, ALU.max))

            def second_expert():
                link(dve.tensor_tensor(r_a[:], r_w2[:], over_e(sec), ALU.is_equal))
                link(dve.tensor_tensor(r_a[:], r_a[:], over_b(rev[:]), ALU.mult))
                link(dve.tensor_reduce(secr, r_a[:], AX.X, ALU.max))

            def pair_indices():
                link(dve.tensor_scalar(pair_e[:, :, 0], bestr, -1.0, float(E), ALU.mult, ALU.add))
                link(dve.tensor_scalar(pair_e[:, :, 1], secr, -1.0, float(E), ALU.mult, ALU.add))
                link(dve.tensor_tensor(esum, best, sec, ALU.add))
                link(dve.reciprocal(rsum, esum))

            def pair_weights():
                link(dve.tensor_tensor(pair_w0[:, :, 0], best, rsum, ALU.mult))
                link(dve.tensor_tensor(pair_w0[:, :, 1], sec, rsum, ALU.mult))
                link(dve.tensor_scalar(pair_w1[:], pair_w0[:], 1.0 - MOE_SCALE, None, ALU.mult))
                dve.scalar_tensor_tensor(out=pair_w[:], in0=pair_w0[:], scalar=MOE_SCALE, in1=pair_w1[:],
                                         op0=ALU.mult, op1=ALU.add).then_inc(route_ready, 1)

            dve.wait_ge(pool_const, 3)
            dve.tensor_reduce(delta16[:], ident[:].rearrange("p (k o) -> p o k", o=OI), AX.X,
                              ALU.add).then_inc(setup_dve, 1)
            dve.wait_ge(setup_dve, 1)
            dve.wait_ge(cond_in, 32)
            dve.tensor_tensor(y_kron[:], cond_rep[:].rearrange("p (b o) -> p b o", o=1).broadcast_to([P, B, OI]),
                              delta16[:].rearrange("p (b o) -> p b o", b=1).broadcast_to([P, B, OI]),
                              ALU.mult).then_inc(kron_ready, 1)
            link(dve.tensor_copy(rev[:], rev_i[:]))
            link(dve.tensor_reduce(cmax, cond_bc[:], AX.X, ALU.max))
            dve.tensor_tensor(r_a[:], cond_bc[:], over_e(cmax), ALU.subtract).then_inc(exp_in_ready, 1)
            top_expert()
            dve.wait_ge(w0_in, 16)
            dve.wait_ge(mask_in, 16)
            dve.tensor_tensor(w0[:], w0[:], mask[:], ALU.mult).then_inc(masked_ready, 1)
            dve.tensor_scalar(cond_rep2[:], cond_rep[:], LORA_SCALE, None, ALU.mult).then_inc(setup_dve, 1)
            def w_lo(k, n):
                dve.wait_ge(whi_done, n)
                dve.tensor_tensor(sh_lo[:, k, :], sh_raw[:, k, :], sh_hi[:, k, :].bitcast(F32),
                                  ALU.subtract).then_inc(wlo_done, 1)

            softmax()
            best_expert()
            dve.wait_ge(wbot_done, 4)
            dve.tensor_copy(wbotT[:, :, 2 * OI:4 * OI].rearrange("p b (a o) -> p a b o", a=2),
                            gu[:, 1, :].rearrange("p (a b o) -> p a b o", a=2, b=B)).then_inc(wbot_dve, 1)
            dve.wait_ge(wbot_done, OB - 1)
            dve.tensor_copy(wbotT[:, :, (OB - 2) * OI:(OB - 1) * OI],
                            gu[:, 3, 0:B * OI].rearrange("p (b o) -> p b o", b=B)).then_inc(wbot_dve, 1)
            w_lo(0, 1)
            w_lo(1, 2)
            dve.wait_ge(l2_in, 16 * 5)

            def x1_out(g):
                c = slice(g * GT, (g + 1) * GT)
                dve.wait_ge(l0_done, g + 1)
                dve.scalar_tensor_tensor(out=xT[:, c], in0=yy[:, g, :], scalar=biases[:, 0:1], in1=xT[:, c],
                                         op0=ALU.add, op1=ALU.add).then_inc(x1_done, 1)

            x1_out(0)
            dve.wait_ge(x1hi_done, 1)
            dve.tensor_tensor(x_lo[:, 0:GT], xT[:, 0:GT], x_hi[:, 0:GT].bitcast(F32), ALU.subtract).then_inc(x1lo_dve, 1)
            x1_out(1)
            x1_out(2)
            w_lo(2, 3)

            def shared_prod(q, par, first):
                dve.wait_ge(sh_gelu_done, q + 1)
                dve.wait_ge(sh_u_done, q + 1)
                if not first:
                    dve.wait_ge(sh_lo_done, q - 1)
                dve.tensor_tensor(prod_s[:, par, :], gelu_s[:, par, :], gu[:, 2 + par, :],
                                  ALU.mult).then_inc(sh_prod_done, 1)

            def shared_lo(q, par, first):
                dve.wait_ge(sh_hi_done, q + 1)
                if not first:
                    dve.wait_ge(sh_dn_done, q - 1)
                dve.tensor_tensor(prod_lo[:, par, :], prod_s[:, par, :], prod_hi[:, par, :].bitcast(F32),
                                  ALU.subtract).then_inc(sh_lo_done, 1)

            def shared_y(g):
                c = bass.ds(g * GT, GT)
                dve.wait_ge(sh_dn_done, (g + 1) * NC)
                dve.tensor_tensor(yT[:, c], yy[:, bass.ds(g, 1), :].rearrange("p a n -> p (a n)"), xT[:, c],
                                  ALU.add).then_inc(sh_y_done, 1)

            def shared_group(g, first, routing=False):
                for c in range(NC):
                    if first and c == 1:
                        shared_lo(0, 0, True)
                    shared_prod(g * NC + c, c % 2, first and c < 2)
                    if not (first and c < 2):
                        shared_lo(g * NC + c - 1, (c - 1) % 2, first and c < 3)
                    if first and c == 0:
                        second_value()
                    if first and c == 1:
                        x1_out(3)
                    if routing and c == 0:
                        second_expert()
                    if routing and c == 1:
                        pair_indices()
                    if routing and c == 3:
                        pair_weights()
                    if not first and c == 2:
                        shared_y(g - 1)

            shared_group(0, True)
            dve.wait_ge(whi_done, 4)
            dve.tensor_tensor(l2_lo[:], l2_raw[:, 0:2, :], l2_hi[:].bitcast(F32), ALU.subtract).then_inc(wlo_done, 1)
            shared_group(1, False, routing=True)
            with dve.Fori(2, NG) as g:
                shared_group(g, False)

            def pair_expert(p):
                return dve.value_load(pair_e_cols[0:1, bass.ds(p, 1)], min_val=0, max_val=E - 1)

            def copy_gu(p, k, e, first):
                if not first:
                    dve.wait_ge(ex_u_done, p - len(pair_gu) + 1)
                dve.tensor_copy(pair_gu[k], sk_gu[:, bass.ds(e, 1), :].rearrange("p a n -> p (a n)")
                                ).then_inc(gu_copied, 1)

            def expert_prod(p, k, first):
                dve.wait_ge(ex_gelu_done, p + 1)
                dve.wait_ge(ex_u_done, p + 1)
                if first:
                    dve.wait_ge(sh_lo_done, NG * NC)
                else:
                    dve.wait_ge(ex_dn_done, p - 1)
                dve.scalar_tensor_tensor(out=prod_s[:, k, :], in0=gelu_s[:, k, :], scalar=pair_w_cols[:, bass.ds(p, 1)],
                                         in1=gu[:, 2 + k, :], op0=ALU.mult, op1=ALU.mult).then_inc(ex_prod_done, 1)

            def x2_out(b, ypar):
                c = bass.ds(b * S, S)
                dve.wait_ge(ex_dn_done, (b + 1) * TOPK)
                dve.tensor_tensor(yT[:, c], yy[:, ypar, 0:S], yT[:, c], ALU.add).then_inc(x2_done, 1)

            def l2_lo_part(g):
                c = bass.ds(g * GT, GT)
                dve.wait_ge(l2_hi_done, g + 1)
                dve.tensor_tensor(x_lo[:, c], yT[:, c], x_hi[:, c].bitcast(F32), ALU.subtract).then_inc(l2_lo_done, 1)

            def l2_scale(g):
                dve.wait_ge(l2_h_done, g + 1)
                dve.tensor_tensor(lora_h[:], yy[:, 2, :].rearrange("p (b s) -> p b s", s=S),
                                  cond_rep2[:, bass.ds(g * BG, BG)].rearrange("p (b o) -> p b o", o=1)
                                  .broadcast_to([P, BG, S]), ALU.mult).then_inc(l2_hs_done, 1)

            def x3_out(g):
                c = bass.ds(g * GT, GT)
                dve.wait_ge(l2_x_done, g + 1)
                dve.scalar_tensor_tensor(out=x3T[:, c], in0=yy[:, 3, :], scalar=biases[:, 1:2], in1=yT[:, c],
                                         op0=ALU.add, op1=ALU.add).then_inc(x3_done, 1)

            def expert_group(g, first=False, last=False):
                for j in range(PG):
                    p = g * PG + j
                    if not (first and j == 0):
                        expert_prod(p - 1, (j - 1) % TOPK, first and j < 3)
                    if not (last and j == PG - 1) and not (first and j == 0):
                        copy_gu(p + 1, (j + 1) % len(pair_gu), pair_expert(p + 1), first and j + 1 < len(pair_gu))
                    if j % 2 == 1 and not (first and j == 1):
                        x2_out(g * BG + (j - 3) // 2, ((j - 3) // 2) % 2)
                    if not first:
                        if j == 2:
                            l2_lo_part(g - 1)
                        elif j == 5:
                            l2_scale(g - 1)
                        elif j == 7:
                            x3_out(g - 1)

            dve.wait_ge(route_ready, 1)
            dve.wait_ge(skill_in, 16 * N_SKILL)
            shared_lo(NG * NC - 1, 1, False)
            copy_gu(1, 1, pair_expert(1), True)
            shared_y(NG - 1)
            dve.wait_ge(sh_y_done, NG)
            dve.wait_ge(setup_dve, 2)
            expert_group(0, first=True)
            with dve.Fori(1, NG - 1) as g:
                expert_group(g)
            expert_group(NG - 1, last=True)

            def hidden3(b, j, first):
                dve.wait_ge(gate3_done, b + 1)
                if not first:
                    dve.wait_ge(dn3_done, b - BG + 1)
                for c in range(NC3):
                    cs = slice(c * S, (c + 1) * S)
                    dve.wait_ge(silu_done, b * NC3 + c + 1)
                    dve.scalar_tensor_tensor(out=hid3[:, j, cs], in0=gu[:, 2 + j % 2, cs],
                                             scalar=bias3[:, bass.ds(b * NB3 + NC3 + c, 1)], in1=silu_s[:, j % 2, cs],
                                             op0=ALU.add, op1=ALU.mult).then_inc(hid3_done, 1)

            def out3(b, j):
                c = bass.ds(b * S, S)
                dve.wait_ge(dn3_done, b + 1)
                dve.scalar_tensor_tensor(out=x3T[:, c], in0=yy[:, j % 2, 0:S], scalar=bias3[:, bass.ds(b * NB3 + 2 * NC3, 1)],
                                         in1=x3T[:, c], op0=ALU.add, op1=ALU.add).then_inc(out_done, 1)

            def l3_group(g, first=False):
                for j in range(BG):
                    b = g * BG + j
                    if not (first and j == 0):
                        hidden3(b - 1, (j - 1) % BG, first)
                    if first and j == 1:
                        x2_out(B - 1, (B - 1) % 2)
                        l2_lo_part(NG - 1)
                    if not (first and j < 3):
                        out3(b - 3, (j - 3) % BG)
                    if first and j == 2:
                        l2_scale(NG - 1)

            expert_prod(NP - 1, TOPK - 1, False)
            dve.wait_ge(b3_copied, B)
            l3_group(0, first=True)
            x3_out(NG - 1)
            with dve.Fori(1, NG) as g:
                l3_group(g)
            hidden3(B - 1, BG - 1, False)
            out3(B - 3, BG - 3)
            out3(B - 2, BG - 2)
            out3(B - 1, BG - 1)


def kernel(x, cond_8, L0_cond_weight, L0_cond_mask, L0_cond_bias, L1_cond_skill_gate, L1_cond_skill_up,
           L1_cond_skill_down, L1_cond_shared_gate, L1_cond_shared_up, L1_cond_shared_down, L2_cond_W_base,
           L2_cond_b_base, L2_cond_As, L2_cond_Bs, L3_cond_W_up, L3_cond_b_up, L3_cond_W_gate, L3_cond_b_gate,
           L3_cond_W_down, L3_cond_b_down):
    import numpy as np
    import concourse.bacc as bacc
    from concourse.bass_utils import run_bass_kernel_spmd

    B, S, D = x.shape
    E = cond_8.shape[1]
    OI = D // E
    H3 = L3_cond_W_up.shape[1]

    def lay(a, *axes):
        a = np.asarray(a)
        return np.ascontiguousarray(a.transpose(*axes) if axes else a)

    def by_partition(b):
        b = np.asarray(b)
        return np.ascontiguousarray(b.reshape(E, -1, D).transpose(2, 0, 1))

    ins = {
        "xT": lay(x, 2, 0, 1).reshape(D, B * S),
        "cond": lay(cond_8),
        "condT": lay(cond_8, 1, 0),
        "w0": lay(np.asarray(L0_cond_weight).reshape(E, D // OI, OI, D), 0, 2, 1, 3).reshape(D, -1),
        "mask": lay(np.asarray(L0_cond_mask).reshape(D // OI, OI, D), 1, 0, 2).reshape(OI, -1),
        "bias0": lay(L0_cond_bias).reshape(D, 1),
        "sk_gate": lay(L1_cond_skill_gate),
        "sk_up": lay(L1_cond_skill_up),
        "sk_down": lay(L1_cond_skill_down),
        "sh_gate": lay(L1_cond_shared_gate),
        "sh_up": lay(L1_cond_shared_up),
        "sh_down": lay(L1_cond_shared_down),
        "wbase": lay(L2_cond_W_base, 1, 0),
        "bbase": lay(L2_cond_b_base).reshape(D, 1),
        "lora_a": lay(L2_cond_As, 2, 0, 1).reshape(D, -1),
        "lora_b": lay(L2_cond_Bs, 0, 2, 1).reshape(D, -1),
        "w3": np.concatenate([
            lay(L3_cond_W_up, 0, 2, 1), lay(L3_cond_W_gate, 0, 2, 1),
            lay(np.asarray(L3_cond_W_down).reshape(E, D, H3 // D, D), 0, 3, 2, 1).reshape(E, D, H3)], axis=2),
        "b3": np.concatenate([by_partition(b) for b in (L3_cond_b_up, L3_cond_b_gate, L3_cond_b_down)], axis=2),
    }
    nc = bacc.Bacc("TRN2", target_bir_lowering=False, num_devices=1)
    aps = [nc.dram_tensor(n + "_dram", a.shape, mybir.dt.from_np(a.dtype), kind="ExternalInput").ap() for n, a in ins.items()]
    out = nc.dram_tensor("outT_dram", (D, B * S), F32, kind="ExternalOutput").ap()
    cond_resid_kernel(nc, *aps, out)
    r = run_bass_kernel_spmd(nc, [{n + "_dram": a for n, a in ins.items()}], core_ids=[0])
    got = r.results[0]["outT_dram"]
    return np.ascontiguousarray(got.reshape(D, B, S).transpose(1, 2, 0))
```
